# Optimizing a Trainium2 kernel written in Bass

```python
import numpy as np
import jax
import jax.numpy as jnp

def _softmax(x, axis=-1):
    return jax.nn.softmax(x, axis=axis)

def _gelu(x):
    return jax.nn.gelu(x, approximate=True)

def _silu(x):
    return jax.nn.silu(x)

def _sigmoid(x):
    return jax.nn.sigmoid(x)

def _layernorm(x, axis=-1, eps=1e-05):
    m = jnp.mean(x, axis=axis, keepdims=True)
    v = jnp.var(x, axis=axis, keepdims=True)
    return (x - m) / jnp.sqrt(v + eps)

def _scatter_add(tgt, idx, src, axis=0):
    return tgt.at[idx].add(src)

def _segment_sum(src, seg, n):
    return jax.ops.segment_sum(src, seg, n)
kernel_name = 'mk_xattn_ffn_d1_seqx_r8_f1d4cc'

def setup_inputs(seed: int=0):
    np.random.seed(seed)
    _w = jnp.asarray

    def _rec_inputs():
        import jax
        import jax.numpy as jnp
        _rk = jax.random.key(seed)
        x = 7.22e-05 + 1 * jax.random.normal(jax.random.fold_in(_rk, 1), (16, 64, 512), jnp.float32)
        _lenS = 64 - jax.random.randint(jax.random.fold_in(_rk, 7), (16,), 0, max(1, 64 // 4) + 1, jnp.int32)
        _lenS2 = 64 - jax.random.randint(jax.random.fold_in(_rk, 8), (16,), 0, max(1, 64 // 4) + 1, jnp.int32)
        _ctx_4096P = jax.random.normal(jax.random.fold_in(_rk, 11), (16, 16, 512), jnp.float32)
        _ctx_4096c = jax.random.dirichlet(jax.random.fold_in(_rk, 511), 0.3 * jnp.ones((16,), jnp.float32), (16, 64))
        _ctx_4096t = jnp.einsum('bsk,bkd->bsd', _ctx_4096c, _ctx_4096P)
        _ctx_4096t = _ctx_4096t * jax.lax.rsqrt(jnp.mean(jnp.square(_ctx_4096t)) + 1e-12) * 0.953939
        ctx_4096 = 4.13588e-05 + 0.999923 * (_ctx_4096t + 0.3 * jax.random.normal(jax.random.fold_in(_rk, 611), (16, 64, 512), jnp.float32))
        fside_Bx32xSxS2_0 = 1.74963e-06 + 0.0200011 * jax.random.normal(jax.random.fold_in(_rk, 13), (16, 32, 64, 64), jnp.float32)
        _validS = jnp.arange(64)[None, :] < _lenS[:, None]
        _validS2 = jnp.arange(64)[None, :] < _lenS2[:, None]
        _causal = jnp.tril(jnp.ones((64, 64), dtype=bool))
        mask_BxSxS2_bk0 = jnp.logical_not(jnp.broadcast_to(_validS2[:, None, :], (16, 64, 64)))
        return (x, ctx_4096, fside_Bx32xSxS2_0, mask_BxSxS2_bk0)
    x, ctx_4096, fside_Bx32xSxS2_0, mask_BxSxS2_bk0 = _rec_inputs()

    def _L0_xattn_setup():
        import jax, jax.numpy as jnp
        import numpy as np
        B, S, D, H, DH = (2, 128, 512, 32, 128)
        key = jax.random.key(seed)
        ks = jax.random.split(key, 7)
        hidden_q = jax.random.normal(ks[0], (B, S, D), dtype=jnp.float32)
        hidden_kv = jax.random.normal(ks[1], (B, S, D), dtype=jnp.float32)
        attention_mask = jnp.tril(jnp.ones((B, S, S), dtype=bool))
        position_bias = jax.random.normal(ks[2], (B, H, S, S), dtype=jnp.float32) * 0.02
        Wq = jax.random.normal(ks[3], (D, H * DH), dtype=jnp.float32) * 0.02
        Wk = jax.random.normal(ks[4], (D, H * DH), dtype=jnp.float32) * 0.02
        Wv = jax.random.normal(ks[5], (D, H * DH), dtype=jnp.float32) * 0.02
        Wo = jax.random.normal(ks[6], (H * DH, D), dtype=jnp.float32) * 0.02
        return {'hidden_q': hidden_q, 'hidden_kv': hidden_kv, 'attention_mask': attention_mask, 'position_bias': position_bias, 'Wq': Wq, 'Wk': Wk, 'Wv': Wv, 'Wo': Wo}
    _L0_xattn_all = _L0_xattn_setup()
    _L0_xattn_in = {k: v for k, v in _L0_xattn_all.items() if k in ('Wq', 'Wk', 'Wv', 'Wo')}
    del _L0_xattn_all

    def _L0_ffn_setup():
        import jax, jax.numpy as jnp
        import numpy as np
        SCALING = 32.0 / 16.0
        key = jax.random.key(seed)
        ks = jax.random.split(key, 7)
        B, T, D, O, R, E = (4, 256, 512, 512, 16, 8)
        x = jax.random.normal(ks[0], (B, T, D), dtype=jnp.float32)
        base_W = jax.random.normal(ks[1], (O, D), dtype=jnp.float32) * D ** (-0.5)
        base_b = jax.random.normal(ks[2], (O,), dtype=jnp.float32) * 0.01
        router_W = jax.random.normal(ks[3], (2 * E - 1, D), dtype=jnp.float32) * D ** (-0.5)
        router_b = jax.random.normal(ks[4], (2 * E - 1,), dtype=jnp.float32) * 0.01
        A = jax.random.normal(ks[5], (E, R, D), dtype=jnp.float32) * D ** (-0.5)
        Bm = jax.random.normal(ks[6], (E, O, R), dtype=jnp.float32) * R ** (-0.5)
        assigned_idx = 0
        others = [i for i in range(E) if i != assigned_idx]
        expert_map = jnp.array([assigned_idx] * E + others, dtype=jnp.int32)
        return {'x': x, 'base_W': base_W, 'base_b': base_b, 'router_W': router_W, 'router_b': router_b, 'A': A, 'B': Bm, 'expert_map': expert_map}
    _L0_ffn_all = _L0_ffn_setup()
    _L0_ffn_in = {k: v for k, v in _L0_ffn_all.items() if k in ('base_W', 'base_b', 'router_W', 'router_b', 'A', 'B', 'expert_map')}
    del _L0_ffn_all
    return {'x': x, 'ctx_4096': ctx_4096, 'fside_Bx32xSxS2_0': fside_Bx32xSxS2_0, 'mask_BxSxS2_bk0': mask_BxSxS2_bk0, 'L0_xattn_Wq': _L0_xattn_in['Wq'], 'L0_xattn_Wk': _L0_xattn_in['Wk'], 'L0_xattn_Wv': _L0_xattn_in['Wv'], 'L0_xattn_Wo': _L0_xattn_in['Wo'], 'L0_ffn_base_W': _L0_ffn_in['base_W'], 'L0_ffn_base_b': _L0_ffn_in['base_b'], 'L0_ffn_router_W': _L0_ffn_in['router_W'], 'L0_ffn_router_b': _L0_ffn_in['router_b'], 'L0_ffn_A': _L0_ffn_in['A'], 'L0_ffn_B': _L0_ffn_in['B'], 'L0_ffn_expert_map': _L0_ffn_in['expert_map']}

def reference(x, ctx_4096, fside_Bx32xSxS2_0, mask_BxSxS2_bk0, L0_xattn_Wq, L0_xattn_Wk, L0_xattn_Wv, L0_xattn_Wo, L0_ffn_base_W, L0_ffn_base_b, L0_ffn_router_W, L0_ffn_router_b, L0_ffn_A, L0_ffn_B, L0_ffn_expert_map):
    import jax
    import jax.numpy as jnp

    def _L0_xattn_ref(hidden_q, hidden_kv, attention_mask, position_bias, Wq, Wk, Wv, Wo):
        import jax, jax.numpy as jnp
        import numpy as np
        B, S, D, H, DH = (2, 128, 512, 32, 128)
        b, lq, _ = hidden_q.shape
        lk = hidden_kv.shape[1]
        h, dh = (H, DH)
        q = (hidden_q @ Wq).reshape(b, lq, h, dh)
        k = (hidden_kv @ Wk).reshape(b, lk, h, dh)
        v = (hidden_kv @ Wv).reshape(b, lk, h, dh)
        scale = 1.0 / jnp.sqrt(jnp.asarray(dh, dtype=q.dtype))
        score = jnp.einsum('bqhd,bkhd->bhqk', q, k) * scale + position_bias
        mask = attention_mask[:, None, :, :]
        neg_inf = jnp.asarray(-jnp.inf, dtype=score.dtype)
        score = jnp.where(mask, score, neg_inf)
        probs = jax.nn.softmax(score, axis=-1)
        probs = jnp.where(mask, probs, jnp.asarray(0, dtype=probs.dtype))
        ctx = jnp.einsum('bhqk,bkhd->bqhd', probs, v).reshape(b, lq, h * dh)
        return ctx @ Wo

    def _L0_ffn_ref(x, base_W, base_b, router_W, router_b, A, B, expert_map):
        import jax, jax.numpy as jnp
        import numpy as np
        SCALING = 32.0 / 16.0
        E = A.shape[0]
        base_out = jnp.einsum('btd,od->bto', x, base_W) + base_b
        logits = jnp.einsum('btd,nd->btn', x, router_W) + router_b
        probs = jax.nn.softmax(logits, axis=-1)
        topk_p, topk_i = jax.lax.top_k(probs, E)
        mapped = expert_map[topk_i]
        onehot = (mapped[..., None] == jnp.arange(E)).astype(x.dtype)
        w = jnp.einsum('btk,btke->bte', topk_p, onehot)
        h = jnp.einsum('btd,erd->bter', x, A)
        lora = jnp.einsum('bter,eor->bto', h * w[..., None], B) * SCALING
        return base_out + lora
    x = x + _L0_xattn_ref(_layernorm(x, axis=-1), ctx_4096, mask_BxSxS2_bk0, fside_Bx32xSxS2_0, L0_xattn_Wq, L0_xattn_Wk, L0_xattn_Wv, L0_xattn_Wo)
    x = x + _L0_ffn_ref(_layernorm(x, axis=-1), L0_ffn_base_W, L0_ffn_base_b, L0_ffn_router_W, L0_ffn_router_b, L0_ffn_A, L0_ffn_B, L0_ffn_expert_map)
    return x

_drawn_inputs = setup_inputs


def setup_inputs(seed=0):
    import zlib

    import numpy as np

    out = dict(_drawn_inputs(seed))
    spreads = {}
    factors = {'fside_Bx32xSxS2_0': 8.0, 'L0_ffn_base_b': 8.0, 'L0_ffn_router_b': 6.813}
    for name, (base, spread) in spreads.items():
        noise = np.random.default_rng([zlib.crc32(name.encode()), seed]).standard_normal(out[name].shape)
        drawn = base * np.exp(spread * noise) if base else spread * noise
        out[name] = jnp.asarray(drawn.astype(out[name].dtype))
    for name, factor in factors.items():
        out[name] = (out[name] * factor).astype(out[name].dtype)
    return out
```

```python
from contextlib import ExitStack

import concourse.bass as bass
from concourse import mybir

F32 = mybir.dt.float32
F32R = mybir.dt.float32r
U32 = mybir.dt.uint32
U8 = mybir.dt.uint8
I32 = mybir.dt.int32
ALU = mybir.AluOpType
ACT = mybir.ActivationFunctionType
AX = mybir.AxisListType

P = 128
B, S, D, H, DH = 16, 64, 512, 32, 128
T = B * S
NT = T // P
DC = D // P
HALF = T // 2
NH = T // HALF
GH = 4
G = H // GH
GD = GH * DH
NB = B // 2
E, R, NR = 8, 16, 15
ER = E * R
ARW = 256
SCALE = float(DH) ** -0.5
LORA_SCALE = 2.0
EPS = 1e-5
NEG = -1e30

OPENING = []
for i in range(NT + 2):
    if i < NT:
        OPENING.append(("ctx", i))
    if i >= 2:
        OPENING.append(("x", i - 2))
    if 1 <= i <= NT:
        OPENING.append(("v", i - 1))
TURNED = [step for step in OPENING if step[0] != "v"]
V0 = NT
P0 = V0 + 2 * NH
PG = GH * 2 * NH + NT
NFW = DC + DC // 2 + 1


def xattn_ffn(nc, x, ctx_in, bias_in, mask_in, Wq, Wk, Wv, Wo, base_W, base_b, router_W, router_b,
              A_in, B_in, emap, out):
    x_d = x.rearrange("(a c) s d -> (c s) a d", c=2)
    ctx_d = ctx_in.rearrange("(a c) s d -> (c s) a d", c=2)
    out_d = out.rearrange("(a c) s d -> (c s) a d", c=2)
    wq_d = Wq.rearrange("(c p) n -> p c n", p=P)
    wk_d = Wk.rearrange("(c p) n -> p c n", p=P)
    wv_d = Wv.rearrange("(c p) n -> c p n", p=P)
    wo_d = Wo.rearrange("(h p) n -> p h n", p=P)
    bw_d = base_W.rearrange("(o p) d -> p o d", p=P)
    a_d = A_in.rearrange("e r d -> (e r) d")
    b_d = B_in.rearrange("e (o p) r -> p o e r", p=P)
    bias_d = bias_in.rearrange("(j f i) h q k -> f i h q j k", f=2, i=2)
    mask_d = mask_in.rearrange("(j f i) q k -> f i q j k", f=2, i=2)

    with ExitStack() as stack:
        def sb(name, shape, dt=F32):
            return stack.enter_context(nc.sbuf_tensor(name, shape, dt))

        def bank(name):
            return stack.enter_context(nc.psum_tensor(name, [P, 512], F32))

        def sem(name):
            return stack.enter_context(nc.semaphore(name))

        xT_hi = sb("xT_hi", [P, DC, T], F32R)
        xT_lo = sb("xT_lo", [P, DC, T], F32R)
        cT_hi = sb("cT_hi", [P, DC * T], F32R)
        cT_lo = sb("cT_lo", [P, DC * T], F32R)
        wq_hi = sb("wq_hi", [P, DC, DH], F32R)
        wq_lo = sb("wq_lo", [P, DC, DH], F32R)
        wk_hi = sb("wk_hi", [P, DC, DH], F32R)
        wk_lo = sb("wk_lo", [P, DC, DH], F32R)
        wv_hi = sb("wv_hi", [P, DC, GD], F32R)
        wv_lo = sb("wv_lo", [P, DC, GD], F32R)
        wo_hi = sb("wo_hi", [P, 2, D], F32R)
        wo_lo = sb("wo_lo", [P, 2, D], F32R)
        oT_hi = sb("oT_hi", [P, 2, T], F32R)
        oT_lo = sb("oT_lo", [P, 2, T], F32R)
        wq_raw = sb("wq_raw", [P, DC, DH])
        wk_raw = sb("wk_raw", [P, DC, DH])
        wv_raw = sb("wv_raw", [P, GD])
        wo_raw = sb("wo_raw", [P, 2, D])
        bw_raw = sb("bw_raw", [P, DC, D])
        a_raw = sb("a_raw", [P, D])
        r_raw = sb("r_raw", [NR, D])
        b_raw = sb("b_raw", [P, DC, ER])
        y = sb("y", [P, NT, D])
        v = sb("v", [P, NT, GD])
        qT = sb("qT", [P, T])
        kT = sb("kT", [P, T])
        bias = sb("bias", [P, NB, S])
        madd = sb("madd", [P, NB, S])
        mask8 = sb("mask8", [P, NB, S], U8)
        some = sb("some", [P, NB])
        sc = sb("sc", [P, NB, S])
        pr = sb("pr", [P, NB, S])
        pT = sb("pT", [P, NT, P])
        mx = sb("mx", [P, NB])
        sm = sb("sm", [P, NB])
        rs = sb("rs", [P, NB])
        ident = sb("ident", [P, P])
        xn = sb("xn", [P, 2, D])
        st = sb("st", [P, 2, 6])
        mv = sb("mv", [P, 2, 2])
        ve = sb("ve", [P, 2])
        rstd = sb("rstd", [P, 2])
        mhalf = sb("mhalf", [P, 1])
        warm = sb("warm", [P, 1])
        bb = sb("bb", [P, D])
        rb = sb("rb", [P, NR])
        mapi = sb("mapi", [P, NR], I32)
        mapf = sb("mapf", [P, NR])
        onehot = sb("onehot", [P, E, NR])
        lg = sb("lg", [P, NR])
        top = sb("top", [P, 8])
        nmax = sb("nmax", [P, 1])
        ex = sb("ex", [P, NR])
        esum = sb("esum", [P, 1])
        rsum = sb("rsum", [P, 1])
        left = sb("left", [P, NR])
        kept = sb("kept", [P, NR])
        ew = sb("ew", [P, E, NR])
        we = sb("we", [P, E])
        wn = sb("wn", [P, E])
        hw = sb("hw", [P, ER])
        hwT_hi = sb("hwT_hi", [P, P], F32R)
        hwT_lo = sb("hwT_lo", [P, P], F32R)

        pP = [bank("pP0"), bank("pP1")]
        pY = [bank("pY0"), bank("pY1")]
        pS = bank("pS")
        pT_ = bank("pT_")
        pO = [bank("pO0"), bank("pO1")]
        pTurn = [pT_, pS, pO[0], pO[1]]

        fw = [t[:, 0:DC * D].rearrange("p (c n) -> p c n", c=DC) for t in (cT_hi, cT_lo)]
        ar = [t[:, DC * D:DC * D + DC * ARW].rearrange("p (c n) -> p c n", c=DC) for t in (cT_hi, cT_lo)]
        bt = [t[:, DC * D + DC * ARW:DC * D + DC * ARW + D] for t in (cT_hi, cT_lo)]
        cTh = cT_hi[:, :].rearrange("p (c t) -> p c t", c=DC)
        cTl = cT_lo[:, :].rearrange("p (c t) -> p c t", c=DC)

        ld_ctx = [sem(f"ld_ctx{i}") for i in range(4)]
        ld_x = [sem(f"ld_x{i}") for i in range(4)]
        ld_wv0 = sem("ld_wv0")
        ld_wq, ld_wk, ld_wv, ld_wo = sem("ld_wq"), sem("ld_wk"), sem("ld_wv"), sem("ld_wo")
        ld_bias = sem("ld_bias")
        ld_mask, ld_small, ld_ffn = sem("ld_mask"), sem("ld_small"), sem("ld_ffn")
        stored = sem("stored")
        made0, made, mask_made, msk, sel_made = sem("made0"), sem("made"), sem("mask_made"), sem("msk"), sem("sel_made")
        warmed = sem("warmed")
        ln_step, ve_made, rstd_made, xn_made = sem("ln_step"), sem("ve_made"), sem("rstd_made"), sem("xn_made")
        turned, turned_hi, turned_lo = sem("turned"), sem("turned_hi"), sem("turned_lo")
        wq_h, wq_l, wk_h, wk_l = sem("wq_h"), sem("wq_l"), sem("wk_h"), sem("wk_l")
        wv_h, wv_l, wo_h, wo_l = sem("wv_h"), sem("wv_l"), sem("wo_h"), sem("wo_l")
        proj_full, proj_free = sem("proj_full"), sem("proj_free")
        bias_made, s_full, s_read = sem("bias_made"), sem("s_full"), sem("s_read")
        sm_step, sub_made, exp_made, p_made = sem("sm_step"), sem("sub_made"), sem("exp_made"), sem("p_made")
        t_full, t_lower, t_upper = sem("t_full"), sem("t_lower"), sem("t_upper")
        o_full, o_hi, o_lo = sem("o_full"), sem("o_hi"), sem("o_lo")
        y_full, y_added = sem("y_full"), sem("y_added")
        fw_full, fw_hi, fw_lo = sem("fw_full"), sem("fw_hi"), sem("fw_lo")
        g_full, r_step, nmax_made, ex_made, hw_made = (sem("g_full"), sem("r_step"), sem("nmax_made"),
                                                       sem("ex_made"), sem("hw_made"))
        hwT_full, hwT_h, hwT_l = sem("hwT_full"), sem("hwT_h"), sem("hwT_l")
        yb_made, f_full, out_made, wn_made = sem("yb_made"), sem("f_full"), sem("out_made"), sem("wn_made")

        block = stack.enter_context(nc.Block())

        def has_next(last, s, ahead):
            return not last or s + ahead < GH

        def turn_of(step):
            n = TURNED.index(step)
            return n, pTurn[(0 if step[0] == "ctx" else 2) + step[1] % 2]

        def ffn_weight(n, part):
            src = pP[n % 2]
            if n < DC:
                return fw[part][:, n, :], src[:, :]
            if n < DC + DC // 2:
                c = 2 * (n - DC)
                return (ar[part][:, c:c + 2, 0:ER + NR],
                        src[:, :].rearrange("p (c n) -> p c n", c=2)[:, :, 0:ER + NR])
            return bt[part], src[:, :]

        @block.sync
        def _(sp):
            def load_qk(h):
                sp.dma_start(wq_raw[:, :, :], wq_d[:, :, bass.ds(h * DH, DH)]).then_inc(ld_wq, 16)

            def load_k(h):
                sp.dma_start(wk_raw[:, :, :], wk_d[:, :, bass.ds(h * DH, DH)]).then_inc(ld_wk, 16)

            def load_bias(h):
                for f in range(2):
                    for i in range(2):
                        sp.dma_start(bias[64 * f:64 * f + 64, i::2, :],
                                     bias_d[f, i, bass.ds(h, 1)].rearrange("o q j k -> (o q) j k")
                                     ).then_inc(ld_bias, 16)

            def load_wo(pair):
                sp.dma_start(wo_raw[:, :, :], wo_d[:, bass.ds(2 * pair, 2), :]).then_inc(ld_wo, 16)

            for i in range(4):
                sp.dma_start(v[:, 2 * i:2 * i + 2, :], ctx_d[:, 2 * i:2 * i + 2, :]).then_inc(ld_ctx[i], 16)
                if i == 0:
                    sp.dma_start(bw_raw[:, :, :], wv_d[:, :, 0:GD].rearrange("c p n -> p c n")).then_inc(ld_wv0, 16)
            load_qk(0)
            load_k(0)
            for f in range(2):
                for i in range(2):
                    sp.dma_start(mask8[64 * f:64 * f + 64, i::2, :], mask_d[f, i]).then_inc(ld_mask, 16)
            load_bias(0)
            load_wo(0)
            sp.dma_start(bb[:, :], base_b.partition_broadcast(P)).then_inc(ld_small, 16)
            sp.dma_start(rb[:, :], router_b.partition_broadcast(P)).then_inc(ld_small, 16)
            sp.dma_start(mapi[:, :], emap.partition_broadcast(P)).then_inc(ld_small, 16)
            for h in (1, 2):
                sp.wait_ge(wq_l, h)
                load_qk(h)
                sp.wait_ge(wk_l, h)
                load_k(h)

            def group(g, last=False):
                for s in range(GH):
                    h = g * GH + s
                    if not last:
                        sp.wait_ge(wv_l, g * GH + (s + GH))
                        sp.dma_start(wv_raw[:, :], wv_d[s, :, bass.ds((g + 1) * GD, GD)]).then_inc(ld_wv, 16)
                    if has_next(last, s, 1):
                        sp.wait_ge(s_read, h + 1)
                        load_bias(h + 1)
                    if has_next(last, s, 3):
                        sp.wait_ge(wq_l, h + 3)
                        load_qk(h + 3)
                    if s % 2 and has_next(last, s, 1):
                        pair = g * 2 + s // 2
                        sp.wait_ge(wo_l, pair + 1)
                        load_wo(pair + 1)
                    if has_next(last, s, 3):
                        sp.wait_ge(wk_l, h + 3)
                        load_k(h + 3)
                    if last and s == 0:
                        sp.dma_start(bw_raw[:, :, :], bw_d).then_inc(ld_ffn, 16)
                        sp.dma_start(a_raw[:, :], a_d).then_inc(ld_ffn, 16)
                        sp.dma_start(r_raw[:, :], router_W).then_inc(ld_ffn, 16)
                        for o in range(DC):
                            sp.dma_start(b_raw[:, o, :].rearrange("p (e r) -> p e r", e=E),
                                         b_d[:, o]).then_inc(ld_ffn, 16)

            group(0)
            with sp.Fori(1, G - 1) as g:
                group(g)
            group(G - 1, last=True)
            for t in range(NT):
                sp.wait_ge(out_made, t + 1)
                sp.dma_start(out_d[:, t, :], y[:, t, :]).then_inc(stored, 16)
            sp.wait_ge(stored, 16 * NT)

        @block.gpsimd
        def _(pool):
            nc.gpsimd.memset(ident[:, :], 0.0).then_inc(made0, 1)
            pool.wait_ge(made0, 1)
            nc.gpsimd.affine_select(out=ident[:, :], in_=ident[:, :], compare_op=ALU.not_equal, fill=1.0,
                                    base=0, pattern=[[-1, P]], channel_multiplier=1).then_inc(made, 1)
            nc.gpsimd.memset(mhalf[:, :], -0.5).then_inc(made0, 1)
            pool.wait_ge(made0, 2)

            def rstd_of(n):
                pool.wait_ge(ve_made, n + 1)
                nc.gpsimd.tensor_tensor(rstd[:, n % 2:n % 2 + 1], ve[:, n % 2:n % 2 + 1], mhalf[:, :],
                                        ALU.pow).then_inc(rstd_made, 1)

            rstd_of(0)
            nc.gpsimd.memset(pT[:, :, :], 0.0).then_inc(made, 1)
            for t in range(1, NT):
                rstd_of(t)

            def add_mask(h):
                pool.wait_ge(ld_bias, (h + 1) * 64)
                nc.gpsimd.tensor_tensor(bias[:, :, :], bias[:, :, :], madd[:, :, :], ALU.add).then_inc(bias_made, 1)

            pool.wait_ge(mask_made, 1)
            for s in range(GH):
                add_mask(s)
            with pool.Fori(1, G) as g:
                for s in range(GH):
                    add_mask(g * GH + s)
            pool.wait_ge(ld_small, 48)
            for t in range(NT):
                rstd_of(NT + t)
                pool.wait_ge(xn_made, NT + t + 1)
                nc.gpsimd.tensor_tensor(y[:, t, :], y[:, t, :], bb[:, :], ALU.add).then_inc(yb_made, 1)

        @block.scalar
        def _(act):
            for i in range(4):
                act.dma_start(y[:, 2 * i:2 * i + 2, :], x_d[:, 2 * i:2 * i + 2, :]).then_inc(ld_x[i], 16)
            act.wait_ge(made0, 2)
            nc.scalar.activation(warm[:, :], mhalf[:, :], ACT.Exp).then_inc(warmed, 1)

            def copy_out(e, dst, src):
                act.wait_ge(proj_full, e + 1)
                nc.scalar.copy(dst, src).then_inc(proj_free, 1)

            def split_q(h):
                act.wait_ge(ld_wq, (h + 1) * 16)
                nc.scalar.copy(wq_hi[:, :, :], wq_raw[:, :, :]).then_inc(wq_h, 1)

            def split_k(h):
                act.wait_ge(ld_wk, (h + 1) * 16)
                nc.scalar.copy(wk_hi[:, :, :], wk_raw[:, :, :]).then_inc(wk_h, 1)

            def project_out(base, half, dst):
                e = base + half
                copy_out(e, dst[:, half % 2 * HALF:half % 2 * HALF + HALF], pP[half % 2][:, :])

            act.wait_ge(ld_wv0, 16)
            for c in range(DC):
                nc.scalar.copy(wv_hi[:, c, :], bw_raw[:, c, :]).then_inc(wv_h, 1)
            for step in OPENING:
                kind, t = step
                if kind == "v":
                    copy_out(t, v[:, t, :], pP[t % 2][:, :])
                    continue
                n, src = turn_of(step)
                dst = xT_hi if kind == "x" else cTh
                act.wait_ge(turned, n + 1)
                nc.scalar.copy(dst[:, :, t * P:(t + 1) * P], src[:, :].rearrange("p (c t) -> p c t", c=DC)
                               ).then_inc(turned_hi, 1)
                if step == ("ctx", 4):
                    split_q(0)
                if step == ("ctx", 6):
                    split_k(0)
            project_out(V0, 0, qT)
            project_out(V0, 1, qT)
            split_q(1)
            project_out(V0, 2, kT)
            project_out(V0, 3, kT)
            split_k(1)

            def group(g, last=False):
                for s in range(GH):
                    h = g * GH + s
                    base = g * PG + (P0 + 2 * NH * s)
                    act.wait_ge(sub_made, h + 1)
                    nc.scalar.activation(pr[:, :, :], sc[:, :, :], ACT.Exp).then_inc(exp_made, 1)
                    if has_next(last, s, 1):
                        project_out(base, 0, qT)
                        project_out(base, 1, qT)
                    elif last:
                        for n in range(NFW):
                            act.wait_ge(fw_full, n + 1)
                            dst, src = ffn_weight(n, 0)
                            if n == NFW - 1:
                                nc.scalar.mul(dst, src, LORA_SCALE).then_inc(fw_hi, 1)
                            else:
                                nc.scalar.copy(dst, src).then_inc(fw_hi, 1)
                    act.wait_ge(t_full, h + 1)
                    nc.scalar.copy(pT[0:64, :, 0:64], pT_[0:64, :].rearrange("p (j q) -> p j q", q=64)
                                   ).then_inc(t_lower, 1)
                    if has_next(last, s, 2):
                        split_q(h + 2)
                    if not last:
                        act.wait_ge(ld_wv, g * 64 + 16 * (s + 1))
                        nc.scalar.copy(wv_hi[:, s, :], wv_raw[:, :]).then_inc(wv_h, 1)
                    if s % 2:
                        act.wait_ge(ld_wo, g * 32 + 16 * (s // 2 + 1))
                        nc.scalar.copy(wo_hi[:, :, :], wo_raw[:, :, :]).then_inc(wo_h, 1)
                    if has_next(last, s, 1):
                        project_out(base, 2, kT)
                        project_out(base, 3, kT)
                    if has_next(last, s, 2):
                        split_k(h + 2)
                    for i in range(NH):
                        act.wait_ge(o_full, h * 2 + (i + 1))
                        nc.scalar.copy(oT_hi[:, s % 2, i * HALF:(i + 1) * HALF], pO[i][:, :]).then_inc(o_hi, 1)
                    if s == GH - 1 and not last:
                        for t in range(NT):
                            copy_out(g * PG + (P0 + GH * 2 * NH + t), v[:, t, :], pP[t % 2][:, :])

            group(0)
            with act.Fori(1, G - 1) as g:
                group(g)
            group(G - 1, last=True)

            for t in range(NT + 1):
                if t < NT:
                    act.wait_ge(turned, 2 * NT + t + 1)
                    nc.scalar.copy(xT_hi[:, :, t * P:(t + 1) * P],
                                   pTurn[t % 2][:, :].rearrange("p (c t) -> p c t", c=DC)).then_inc(turned_hi, 1)
                if t >= 1:
                    act.wait_ge(nmax_made, t)
                    nc.scalar.activation(ex[:, :], lg[:, :], ACT.Exp, bias=nmax[:, 0:1],
                                         accum_out=esum[:, 0:1]).then_inc(ex_made, 1)
                    act.wait_ge(hwT_full, t)
                    nc.scalar.copy(hwT_hi[:, :], pO[1][:, 0:P]).then_inc(hwT_h, 1)

        @block.vector
        def _(dve):
            def lower(dst, src, hi, done):
                nc.vector.tensor_tensor(dst, src, hi.bitcast(F32), ALU.subtract).then_inc(done, 1)

            def split_q(h):
                dve.wait_ge(wq_h, h + 1)
                lower(wq_lo[:, :, :], wq_raw[:, :, :], wq_hi[:, :, :], wq_l)

            def split_k(h):
                dve.wait_ge(wk_h, h + 1)
                lower(wk_lo[:, :, :], wk_raw[:, :, :], wk_hi[:, :, :], wk_l)

            def stats(n, t):
                b = n % 2
                nc.vector.bn_stats(st[:, b, :], y[:, t, :]).then_inc(ln_step, 1)
                dve.wait_ge(ln_step, 2 * n + 1)
                nc.vector.bn_aggr(mv[:, b, :], st[:, b, :]).then_inc(ln_step, 1)
                dve.wait_ge(ln_step, 2 * n + 2)
                nc.vector.tensor_scalar(ve[:, b:b + 1], mv[:, b, 1:2], EPS, None, ALU.add).then_inc(ve_made, 1)

            def normalise(n, t):
                b = n % 2
                dve.wait_ge(rstd_made, n + 1)
                if n >= 2:
                    dve.wait_ge(turned, turned_before(n))
                nc.vector.tensor_scalar(xn[:, b, :], y[:, t, :], mv[:, b, 0:1], rstd[:, b:b + 1],
                                        ALU.subtract, ALU.mult).then_inc(xn_made, 1)

            def turned_before(n):
                m = n - 2
                return (TURNED.index(("x", m)) if m < NT else NT + m) + 1

            dve.wait_ge(ld_x[0], 16)
            stats(0, 0)
            stats(1, 1)
            normalise(0, 0)
            dve.wait_ge(ld_wv0, 16)
            for c in range(DC):
                dve.wait_ge(wv_h, c + 1)
                lower(wv_lo[:, c, :], bw_raw[:, c, :], wv_hi[:, c, :], wv_l)
            for step in OPENING:
                kind, t = step
                if kind == "v":
                    if t + 2 < NT:
                        if t % 2 == 0:
                            dve.wait_ge(ld_x[t // 2 + 1], 16)
                        stats(t + 2, t + 2)
                    if t + 1 < NT:
                        normalise(t + 1, t + 1)
                    continue
                n, src = turn_of(step)
                hi, lo = (xT_hi, xT_lo) if kind == "x" else (cTh, cTl)
                dve.wait_ge(turned_hi, n + 1)
                lower(lo[:, :, t * P:(t + 1) * P], src[:, :].rearrange("p (c t) -> p c t", c=DC),
                      hi[:, :, t * P:(t + 1) * P], turned_lo)
                if step == ("ctx", 4):
                    split_q(0)
                if step == ("ctx", 6):
                    split_k(0)
            dve.wait_ge(ld_mask, 64)
            nc.vector.tensor_scalar(madd[:, :, :], mask8[:, :, :], -NEG, NEG, ALU.mult, ALU.add).then_inc(mask_made, 1)
            nc.vector.tensor_reduce(some[:, :], mask8[:, :, :], AX.X, ALU.max).then_inc(msk, 1)
            dve.wait_ge(ld_small, 48)
            nc.vector.tensor_copy(mapf[:, :], mapi[:, :]).then_inc(msk, 1)
            dve.wait_ge(msk, 2)
            for e in range(E):
                nc.vector.tensor_scalar(onehot[:, e, :], mapf[:, :], float(e), None, ALU.is_equal).then_inc(sel_made, 1)
            split_q(1)
            split_k(1)

            def group(g, first=False, last=False):
                for s in range(GH):
                    h = g * GH + s
                    step = h * 4
                    dve.wait_ge(s_full, h + 1)
                    dve.wait_ge(bias_made, h + 1)
                    nc.vector.scalar_tensor_tensor(out=sc[:, :, :], in0=pS[:, :].rearrange("p (b k) -> p b k", k=S),
                                                   scalar=SCALE, in1=bias[:, :, :], op0=ALU.mult,
                                                   op1=ALU.add).then_inc(s_read, 1)
                    dve.wait_ge(s_read, h + 1)
                    nc.vector.tensor_reduce(mx[:, :], sc[:, :, :], AX.X, ALU.max).then_inc(sm_step, 1)
                    dve.wait_ge(sm_step, step + 1)
                    nc.vector.tensor_tensor(sc[:, :, :], sc[:, :, :],
                                            mx[:, :].unsqueeze(2).to_broadcast([P, NB, S]),
                                            ALU.subtract).then_inc(sub_made, 1)
                    dve.wait_ge(exp_made, h + 1)
                    nc.vector.tensor_reduce(sm[:, :], pr[:, :, :], AX.X, ALU.add).then_inc(sm_step, 1)
                    dve.wait_ge(sm_step, step + 2)
                    nc.vector.reciprocal(rs[:, :], sm[:, :]).then_inc(sm_step, 1)
                    dve.wait_ge(sm_step, step + 3)
                    nc.vector.tensor_tensor(rs[:, :], rs[:, :], some[:, :], ALU.mult).then_inc(sm_step, 1)
                    dve.wait_ge(sm_step, step + 4)
                    nc.vector.tensor_tensor(pr[:, :, :], pr[:, :, :],
                                            rs[:, :].unsqueeze(2).to_broadcast([P, NB, S]),
                                            ALU.mult).then_inc(p_made, 1)
                    if last and s == GH - 1:
                        for part in range(2):
                            for c in range(DC):
                                nc.vector.memset(ar[part][:, c, ER + NR:ARW].bitcast(U32), 0).then_inc(sel_made, 1)
                        for n in range(NFW):
                            dve.wait_ge(fw_hi, n + 1)
                            dst, src = ffn_weight(n, 1)
                            hi, _ = ffn_weight(n, 0)
                            if n == NFW - 1:
                                nc.vector.scalar_tensor_tensor(out=dst, in0=src, scalar=LORA_SCALE,
                                                               in1=hi.bitcast(F32), op0=ALU.mult,
                                                               op1=ALU.subtract).then_inc(fw_lo, 1)
                            else:
                                lower(dst, src, hi, fw_lo)
                    dve.wait_ge(t_full, h + 1)
                    nc.vector.tensor_copy(pT[64:128, :, 64:128], pT_[64:128, :].rearrange("p (j q) -> p j q", q=64)
                                          ).then_inc(t_upper, 1)
                    if has_next(last, s, 2):
                        split_q(h + 2)
                    if not last:
                        dve.wait_ge(wv_h, g * GH + (GH + s + 1))
                        lower(wv_lo[:, s, :], wv_raw[:, :], wv_hi[:, s, :], wv_l)
                    if s % 2:
                        dve.wait_ge(wo_h, g * 2 + (s // 2 + 1))
                        lower(wo_lo[:, :, :], wo_raw[:, :, :], wo_hi[:, :, :], wo_l)
                    if has_next(last, s, 2):
                        split_k(h + 2)
                    if s % 2 == 0 and not (first and s == 0):
                        add_y(g * 2 + (s // 2 - 1))
                    for i in range(NH):
                        dve.wait_ge(o_hi, h * 2 + (i + 1))
                        lower(oT_lo[:, s % 2, i * HALF:(i + 1) * HALF], pO[i][:, :],
                              oT_hi[:, s % 2, i * HALF:(i + 1) * HALF], o_lo)

            def add_tile(pair, t):
                dve.wait_ge(y_full, pair * NT + (t + 1))
                nc.vector.tensor_tensor(y[:, t, :], y[:, t, :], pY[t % 2][:, :], ALU.add).then_inc(y_added, 1)

            def add_y(pair):
                for t in range(NT):
                    add_tile(pair, t)

            group(0, first=True)
            with dve.Fori(1, G - 1) as g:
                group(g)
            group(G - 1, last=True)

            last_pair = H // 2 - 1
            dve.wait_ge(sel_made, E + 2 * DC)

            def chain(ins, n):
                ins.then_inc(r_step, 1)
                dve.wait_ge(r_step, n + 1)

            def route(t):
                n = 8 * t
                dve.wait_ge(g_full, t + 1)
                chain(nc.vector.tensor_tensor(lg[:, :], pO[0][:, ER:ER + NR], rb[:, :], ALU.add), n)
                chain(nc.vector.max(top[:, :], lg[:, :]), n + 1)
                nc.vector.tensor_scalar(nmax[:, :], top[:, 0:1], -1.0, None, ALU.mult).then_inc(nmax_made, 1)
                dve.wait_ge(ex_made, t + 1)
                chain(nc.vector.max(top[:, :], ex[:, :]), n + 2)
                chain(nc.vector.match_replace(left[:, :], top[:, :], ex[:, :], -1.0), n + 3)
                chain(nc.vector.scalar_tensor_tensor(out=kept[:, :], in0=left[:, :], scalar=0.0, in1=ex[:, :],
                                                     op0=ALU.is_lt, op1=ALU.mult), n + 4)
                nc.vector.tensor_tensor(ew[:, :, :], onehot[:, :, :],
                                        kept[:, :].unsqueeze(1).to_broadcast([P, E, NR]), ALU.mult
                                        ).then_inc(r_step, 1)
                chain(nc.vector.reciprocal(rsum[:, :], esum[:, :]), n + 6)
                chain(nc.vector.tensor_reduce(we[:, :], ew[:, :, :], AX.X, ALU.add), n + 7)
                nc.vector.tensor_scalar(wn[:, :], we[:, :], rsum[:, 0:1], None, ALU.mult).then_inc(wn_made, 1)
                dve.wait_ge(wn_made, t + 1)
                nc.vector.tensor_tensor(hw[:, :].rearrange("p (e r) -> p e r", e=E),
                                        pO[0][:, 0:ER].rearrange("p (e r) -> p e r", e=E),
                                        wn[:, :].unsqueeze(2).to_broadcast([P, E, R]), ALU.mult
                                        ).then_inc(hw_made, 1)

            def turn_lo(t):
                dve.wait_ge(turned_hi, 2 * NT + t + 1)
                lower(xT_lo[:, :, t * P:(t + 1) * P], pTurn[t % 2][:, :].rearrange("p (c t) -> p c t", c=DC),
                      xT_hi[:, :, t * P:(t + 1) * P], turned_lo)

            def finish(t):
                dve.wait_ge(hwT_h, t + 1)
                lower(hwT_lo[:, :], pO[1][:, 0:P], hwT_hi[:, :], hwT_l)

            def give(t):
                dve.wait_ge(f_full, t + 1)
                dve.wait_ge(yb_made, t + 1)
                nc.vector.tensor_tensor(y[:, t, :], y[:, t, :], pP[t % 2][:, :], ALU.add).then_inc(out_made, 1)

            for t in range(NT + 2):
                if t < NT:
                    add_tile(last_pair, t)
                    dve.wait_ge(y_added, last_pair * NT + t + 1)
                    stats(NT + t, t)
                    normalise(NT + t, t)
                    turn_lo(t)
                if 1 <= t <= NT:
                    route(t - 1)
                    finish(t - 1)
                if t >= 2:
                    give(t - 2)

        @block.tensor
        def _(pe):
            def product(bank_, pairs, first=True, last=True):
                terms = [(a[i], b[j]) for i, j in ((0, 0), (1, 0), (0, 1)) for a, b in pairs]
                for n, (a, b) in enumerate(terms):
                    mm = nc.tensor.matmul(bank_, a, b, start=first and n == 0, stop=last and n == len(terms) - 1)
                return mm

            def project(e, n, w, xt, half):
                if not isinstance(e, int) or e >= 2:
                    pe.wait_ge(proj_free, e - 1)
                cols = slice(half * HALF, (half + 1) * HALF)
                product(pP[n % 2][:, :], [((w[0][:, c, :], w[1][:, c, :]), (xt[0][:, c, cols], xt[1][:, c, cols]))
                                          for c in range(DC)]).then_inc(proj_full, 1)

            def v_tile(e, t):
                if not isinstance(e, int) or e >= 2:
                    pe.wait_ge(proj_free, e - 1)
                cols = slice(t * P, (t + 1) * P)
                product(pP[t % 2][:, :], [((cTh[:, c, cols], cTl[:, c, cols]), (wv_hi[:, c, :], wv_lo[:, c, :]))
                                          for c in range(DC)]).then_inc(proj_full, 1)

            def turn(n, src, dst):
                for c in range(DC):
                    mm = nc.tensor.transpose(dst[:, c * P:(c + 1) * P], src[:, c * P:(c + 1) * P], ident[:, :])
                mm.then_inc(turned, 1)

            WQ, WK = (wq_hi, wq_lo), (wk_hi, wk_lo)
            XT, CT = (xT_hi, xT_lo), (cTh, cTl)

            pe.wait_ge(made, 1)
            for step in OPENING:
                kind, t = step
                if kind == "v":
                    pe.wait_ge(turned_lo, TURNED.index(("ctx", t)) + 1)
                    pe.wait_ge(wv_l, DC)
                    v_tile(t, t)
                    continue
                n, dst = turn_of(step)
                if t >= 2:
                    pe.wait_ge(turned_lo, TURNED.index((kind, t - 2)) + 1)
                if kind == "ctx":
                    if t % 2 == 0:
                        pe.wait_ge(ld_ctx[t // 2], 16)
                    turn(n, v[:, t, :], dst)
                else:
                    pe.wait_ge(xn_made, t + 1)
                    turn(n, xn[:, t % 2, :], dst)
            pe.wait_ge(turned_lo, 2 * NT)
            pe.wait_ge(wq_l, 1)
            for half in range(NH):
                project(V0 + half, half, WQ, XT, half)
            pe.wait_ge(wk_l, 1)
            for half in range(NH):
                project(V0 + NH + half, half, WK, CT, half)

            def times_wo(pair, t):
                cols = slice(t * P, (t + 1) * P)
                product(pY[t % 2][:, :], [((oT_hi[:, i, cols], oT_lo[:, i, cols]), (wo_hi[:, i, :], wo_lo[:, i, :]))
                                          for i in range(2)]).then_inc(y_full, 1)

            def group(g, first=False, last=False):
                for s in range(GH):
                    h = g * GH + s
                    base = g * PG + (P0 + 2 * NH * s)
                    if s == 0:
                        pe.wait_ge(proj_free, P0 if first else g * PG + (P0 - NT))
                    else:
                        pe.wait_ge(proj_free, base)
                    for half in range(2):
                        for b in [b for b in range(B) if b // 2 % 2 == half]:
                            blk = 2 * (b // 4) + b % 2
                            mm = nc.tensor.matmul(pS[64 * half:64 * half + 64, blk * S:(blk + 1) * S],
                                                  qT[:, b * S:(b + 1) * S], kT[:, b * S:(b + 1) * S],
                                                  start=True, stop=True)
                    mm.then_inc(s_full, 1)
                    if has_next(last, s, 1):
                        pe.wait_ge(wq_l, h + 2)
                        for half in range(NH):
                            project(base + half, half, WQ, XT, half)
                    elif last:
                        ffn_weights()
                    pe.wait_ge(p_made, h + 1)
                    for j in range(NB // 2):
                        mm = nc.tensor.transpose(pT_[:, j * P:(j + 1) * P],
                                                 pr[:, 2 * j:2 * j + 2, :].rearrange("p a k -> p (a k)"), ident[:, :])
                    mm.then_inc(t_full, 1)
                    if has_next(last, s, 1):
                        pe.wait_ge(wk_l, h + 2)
                        for half in range(NH):
                            project(base + (NH + half), half, WK, CT, half)
                    if s % 2 == 0 and not (first and s == 0):
                        pair = g * 2 + (s // 2 - 1)
                        pe.wait_ge(wo_l, pair + 1)
                        pe.wait_ge(o_lo, h * 2)
                        for t in range(NT):
                            if not (first and s == 2 and t < 2):
                                pe.wait_ge(y_added, pair * NT + (t - 1))
                            times_wo(pair, t)
                    pe.wait_ge(t_lower, h + 1)
                    pe.wait_ge(t_upper, h + 1)
                    if not (first and s == 0):
                        pe.wait_ge(o_lo, h * 2)
                    if s == 0:
                        pe.wait_ge(proj_free, g * PG + P0)
                        if first:
                            pe.wait_ge(made, 2)
                    for i in range(NH):
                        for q in range(NT // 2):
                            t = i * (NT // 2) + q
                            mm = nc.tensor.matmul(pO[i][:, q * P:(q + 1) * P], v[:, t, s * DH:(s + 1) * DH],
                                                  pT[:, t, :], start=True, stop=True)
                        mm.then_inc(o_full, 1)
                    if s == GH - 1 and not last:
                        pe.wait_ge(wv_l, g * GH + 2 * GH)
                        for t in range(NT):
                            v_tile(g * PG + (P0 + GH * 2 * NH + t), t)

            def ffn_weights():
                pe.wait_ge(ld_ffn, 16 * (3 + DC))
                for n in range(NFW):
                    dst = pP[n % 2]
                    if n >= 2:
                        pe.wait_ge(fw_lo, n - 1)
                    else:
                        pe.wait_ge(proj_free, P0 + (G - 1) * PG + 3 * 2 * NH)
                    if n < DC:
                        for o in range(DC):
                            mm = nc.tensor.transpose(dst[:, o * P:(o + 1) * P], bw_raw[:, o, n * P:(n + 1) * P],
                                                     ident[:, :])
                    elif n < NFW - 1:
                        for i in range(2):
                            c = 2 * (n - DC) + i
                            nc.tensor.transpose(dst[:, i * ARW:i * ARW + ER], a_raw[:, c * P:(c + 1) * P],
                                                ident[:, :])
                            mm = nc.tensor.transpose(dst[:, i * ARW + ER:i * ARW + ER + NR],
                                                     r_raw[:, c * P:(c + 1) * P], ident[0:NR, 0:NR])
                    else:
                        for o in range(DC):
                            mm = nc.tensor.transpose(dst[:, o * P:(o + 1) * P], b_raw[:, o, :], ident[:, :])
                    mm.then_inc(fw_full, 1)

            group(0, first=True)
            with pe.Fori(1, G - 1) as g:
                group(g)
            group(G - 1, last=True)

            last_pair = H // 2 - 1

            def last_wo(t):
                pe.wait_ge(y_added, last_pair * NT + t - 1)
                times_wo(last_pair, t)

            def lora(t):
                pe.wait_ge(hw_made, t + 1)
                nc.tensor.transpose(pO[1][:, 0:P], hw[:, :], ident[:, :]).then_inc(hwT_full, 1)
                pe.wait_ge(hwT_l, t + 1)
                product(pP[t % 2][:, :], [((hwT_hi[:, :], hwT_lo[:, :]), bt)], first=False).then_inc(f_full, 1)

            pe.wait_ge(wo_l, last_pair + 1)
            pe.wait_ge(o_lo, 2 * H)
            for t in range(NT + 1):
                if t == 0:
                    for i in range(3):
                        last_wo(i)
                elif t + 2 < NT:
                    last_wo(t + 2)
                if t < NT:
                    cols = slice(t * P, (t + 1) * P)
                    pe.wait_ge(xn_made, NT + t + 1)
                    if t >= 2:
                        pe.wait_ge(turned_lo, 2 * NT + t - 1)
                    turn(2 * NT + t, xn[:, t % 2, :], pTurn[t % 2])
                if t >= 1:
                    lora(t - 1)
                if t < NT:
                    pe.wait_ge(turned_lo, 2 * NT + t + 1)
                    if t == 0:
                        pe.wait_ge(fw_lo, NFW)
                        pe.wait_ge(sel_made, E + 2 * DC)
                    xt = [(xT_hi[:, c, cols], xT_lo[:, c, cols]) for c in range(DC)]
                    product(pO[0][:, 0:ARW], [(xt[c], (ar[0][:, c, :], ar[1][:, c, :])) for c in range(DC)]
                            ).then_inc(g_full, 1)
                    if t >= 2:
                        pe.wait_ge(out_made, t - 1)
                    product(pP[t % 2][:, :], [(xt[c], (fw[0][:, c, :], fw[1][:, c, :])) for c in range(DC)],
                            last=False)


_INS = ["x", "ctx_4096", "fside_Bx32xSxS2_0", "mask_BxSxS2_bk0", "L0_xattn_Wq", "L0_xattn_Wk", "L0_xattn_Wv",
        "L0_xattn_Wo", "L0_ffn_base_W", "L0_ffn_base_b", "L0_ffn_router_W", "L0_ffn_router_b", "L0_ffn_A",
        "L0_ffn_B", "L0_ffn_expert_map"]


def kernel(**inputs):
    import numpy as _np
    import concourse.bacc as _bacc
    from concourse import mybir as _mybir
    from concourse.bass_utils import run_bass_kernel_spmd as _run

    nc = _bacc.Bacc("TRN2", target_bir_lowering=False, num_devices=1)
    arrays, args = {}, []
    for name in _INS:
        a = _np.ascontiguousarray(inputs[name])
        arrays[f"in_{name}"] = a
        args.append(nc.dram_tensor(f"in_{name}", a.shape, _mybir.dt.from_np(a.dtype), kind="ExternalInput").ap())
    out = nc.dram_tensor("out_0", (B, S, D), _mybir.dt.float32, kind="ExternalOutput").ap()
    xattn_ffn(nc, *args, out)
    r = _run(nc, [arrays], core_ids=[0])
    return r.results[0]["out_0"]
```

```python
from contextlib import ExitStack

import concourse.bass as bass
from concourse import mybir

F32 = mybir.dt.float32
F32R = mybir.dt.float32r
U32 = mybir.dt.uint32
U8 = mybir.dt.uint8
I32 = mybir.dt.int32
ALU = mybir.AluOpType
ACT = mybir.ActivationFunctionType
AX = mybir.AxisListType

P = 128
B, S, D, H, DH = 16, 64, 512, 32, 128
T = B * S
NT = T // P
DC = D // P
HALF = T // 2
NH = T // HALF
GH = 4
G = H // GH
GD = GH * DH
NB = B // 2
E, R, NR = 8, 16, 15
ER = E * R
ARW = 256
SCALE = float(DH) ** -0.5
LORA_SCALE = 2.0
EPS = 1e-5
NEG = -1e30

OPENING = []
for i in range(NT + 2):
    if i < NT:
        OPENING.append(("ctx", i))
    if i >= 2:
        OPENING.append(("x", i - 2))
    if 1 <= i < NT:
        OPENING.append(("v", i - 1))
OPENING += [("k", 0), ("k", 1), ("q", 0), ("q", 1), ("v", NT - 1)]
TURNED = [step for step in OPENING if step[0] in ("ctx", "x")]
PROJECTED = [step for step in OPENING if step not in TURNED]
P0 = len(PROJECTED)
PG = GH * 2 * NH + NT
NFW = DC + DC // 2 + 1
NRB = NT // 2
RB = 11


def xattn_ffn(nc, x, ctx_in, bias_in, mask_in, Wq, Wk, Wv, Wo, base_W, base_b, router_W, router_b,
              A_in, B_in, emap, out):
    x_d = x.rearrange("(a c) s d -> (c s) a d", c=2)
    ctx_d = ctx_in.rearrange("(a c) s d -> (c s) a d", c=2)
    out_d = out.rearrange("(a c) s d -> (c s) a d", c=2)
    wq_d = Wq.rearrange("(c p) n -> p c n", p=P)
    wk_d = Wk.rearrange("(c p) n -> p c n", p=P)
    wv_d = Wv.rearrange("(c p) n -> c p n", p=P)
    wo_d = Wo.rearrange("(h p) n -> p h n", p=P)
    bw_d = base_W.rearrange("(o p) d -> p o d", p=P)
    a_d = A_in.rearrange("e r d -> (e r) d")
    b_d = B_in.rearrange("e (o p) r -> p o e r", p=P)
    bias_d = bias_in.rearrange("(j f i) h q k -> f i h q j k", f=2, i=2)
    mask_d = mask_in.rearrange("(j f i) q k -> f i q j k", f=2, i=2)

    with ExitStack() as stack:
        def sb(name, shape, dt=F32):
            return stack.enter_context(nc.sbuf_tensor(name, shape, dt))

        def bank(name):
            return stack.enter_context(nc.psum_tensor(name, [P, 512], F32))

        def sem(name):
            return stack.enter_context(nc.semaphore(name))

        xT_hi = sb("xT_hi", [P, DC, T], F32R)
        xT_lo = sb("xT_lo", [P, DC, T], F32R)
        cT_hi = sb("cT_hi", [P, DC * T], F32R)
        cT_lo = sb("cT_lo", [P, DC * T], F32R)
        wq_hi = sb("wq_hi", [P, DC, DH], F32R)
        wq_lo = sb("wq_lo", [P, DC, DH], F32R)
        wk_hi = sb("wk_hi", [P, DC, DH], F32R)
        wk_lo = sb("wk_lo", [P, DC, DH], F32R)
        wv_hi = sb("wv_hi", [P, DC, GD], F32R)
        wv_lo = sb("wv_lo", [P, DC, GD], F32R)
        wo_hi = sb("wo_hi", [P, 2, D], F32R)
        wo_lo = sb("wo_lo", [P, 2, D], F32R)
        oT_hi = sb("oT_hi", [P, 2, T], F32R)
        oT_lo = sb("oT_lo", [P, 2, T], F32R)
        wq_raw = sb("wq_raw", [P, DC, DH])
        wk_raw = sb("wk_raw", [P, DC, DH])
        wv_raw = sb("wv_raw", [P, GD])
        wo_raw = sb("wo_raw", [P, 2, D])
        bw_raw = sb("bw_raw", [P, DC, D])
        a_raw = sb("a_raw", [P, D])
        r_raw = sb("r_raw", [NR, D])
        b_raw = sb("b_raw", [P, DC, ER])
        y = sb("y", [P, NT, D])
        v = sb("v", [P, NT, GD])
        qT = sb("qT", [P, T])
        kT = sb("kT", [P, T])
        bias = sb("bias", [P, NB, S])
        madd = sb("madd", [P, NB, S])
        mask8 = sb("mask8", [P, NB, S], U8)
        some = sb("some", [P, NB])
        sc = sb("sc", [P, NB, S])
        pr = sb("pr", [P, NB, S])
        pT = sb("pT", [P, NT, P])
        mx = sb("mx", [P, NB])
        sm = sb("sm", [P, NB])
        rs = sb("rs", [P, NB])
        ident = sb("ident", [P, P])
        xn = sb("xn", [P, 2, D])
        st = sb("st", [P, 2, 6])
        mv = sb("mv", [P, 2, 2])
        ve = sb("ve", [P, 2])
        rstd = sb("rstd", [P, 2])
        mhalf = sb("mhalf", [P, 1])
        warm = sb("warm", [P, 1])
        bb = sb("bb", [P, D])
        rb = sb("rb", [P, NR])
        mapi = sb("mapi", [P, NR], I32)
        mapf = sb("mapf", [P, NR])
        onehot = sb("onehot", [P, E, NR])
        lg = sb("lg", [P, NT, NR])
        lmax = sb("lmax", [P, NT])
        top = sb("top", [P, NT, 8])
        ex = sb("ex", [P, NT, NR])
        esum = sb("esum", [P, NT])
        rsum = sb("rsum", [P, NT])
        left = sb("left", [P, NT, NR])
        kept = sb("kept", [P, NT, NR])
        ew = sb("ew", [P, NRB, E, NR])
        we = sb("we", [P, NT, E])
        wn = sb("wn", [P, NT, E])
        hw = sb("hw", [P, NT, ER])
        hwT_hi = sb("hwT_hi", [P, 2, P], F32R)
        hwT_lo = sb("hwT_lo", [P, 2, P], F32R)

        pP = [bank("pP0"), bank("pP1")]
        pY = [bank("pY0"), bank("pY1")]
        pS = bank("pS")
        pT_ = bank("pT_")
        pO = [bank("pO0"), bank("pO1")]
        pTurn = [pT_, pS, pO[0], pO[1]]

        pG = [pO[0], pO[1], pY[0], pY[1]]

        pF = [pP[0], pP[1], pO[0]]

        fw = (wv_hi, wv_lo)
        last_oT = [t[:, 0:2 * T].rearrange("p (i t) -> p i t", i=2) for t in (cT_hi, cT_lo)]
        ar = [t[:, 2 * T:2 * T + DC * ARW].rearrange("p (c n) -> p c n", c=DC) for t in (cT_hi, cT_lo)]
        bt = [t[:, 2 * T + DC * ARW:2 * T + DC * ARW + D] for t in (cT_hi, cT_lo)]
        last_wo = [[w[:, :, :].rearrange("p c n -> p (c n)") for w in pair]
                   for pair in ((wq_hi, wk_hi), (wq_lo, wk_lo))]
        cTh = cT_hi[:, :].rearrange("p (c t) -> p c t", c=DC)
        cTl = cT_lo[:, :].rearrange("p (c t) -> p c t", c=DC)

        ld_ctx = [sem(f"ld_ctx{i}") for i in range(NT)]
        ld_x = [sem(f"ld_x{i}") for i in range(NT)]
        ld_wv0 = [sem(f"ld_wv0_{c}") for c in range(DC)]
        ld_wq, ld_wk, ld_wv, ld_wo = sem("ld_wq"), sem("ld_wk"), sem("ld_wv"), sem("ld_wo")
        ld_bias = sem("ld_bias")
        ld_mask, ld_small, ld_ffn = sem("ld_mask"), sem("ld_small"), sem("ld_ffn")
        stored = sem("stored")
        made0, made, mask_made, msk, sel_made = sem("made0"), sem("made"), sem("mask_made"), sem("msk"), sem("sel_made")
        warmed = sem("warmed")
        ln_step, ve_made, rstd_made, xn_made = sem("ln_step"), sem("ve_made"), sem("rstd_made"), sem("xn_made")
        turned, turned_hi, turned_lo = sem("turned"), sem("turned_hi"), sem("turned_lo")
        wq_h, wq_l, wk_h, wk_l = sem("wq_h"), sem("wq_l"), sem("wk_h"), sem("wk_l")
        wv_h, wv_l, wo_h, wo_l = sem("wv_h"), sem("wv_l"), sem("wo_h"), sem("wo_l")
        proj_full, proj_free = sem("proj_full"), sem("proj_free")
        bias_made, s_full, s_read = sem("bias_made"), sem("s_full"), sem("s_read")
        sm_step, sub_made, exp_made, p_made = sem("sm_step"), sem("sub_made"), sem("exp_made"), sem("p_made")
        t_full, t_lower, t_upper = sem("t_full"), sem("t_lower"), sem("t_upper")
        o_full, o_hi, o_lo = sem("o_full"), sem("o_hi"), sem("o_lo")
        y_full, y_added = sem("y_full"), sem("y_added")
        fw_full, fw_hi, fw_lo = sem("fw_full"), sem("fw_hi"), sem("fw_lo")
        g_full, r_step, lg_made, ex_made, hw_made = (sem("g_full"), sem("r_step"), sem("lg_made"),
                                                     sem("ex_made"), sem("hw_made"))
        hwT_full, hwT_h, hwT_l = sem("hwT_full"), sem("hwT_h"), sem("hwT_l")
        yb_made, f_full, out_made = sem("yb_made"), sem("f_full"), sem("out_made")

        block = stack.enter_context(nc.Block())

        def has_next(last, s, ahead):
            return not last or s + ahead < GH

        def turn_of(step):
            n = TURNED.index(step)
            return n, pTurn[(0 if step[0] == "ctx" else 2) + step[1] % 2]

        def ffn_weight(n, part):
            src = (pY if n < DC else pP)[n % 2]
            if n < DC:
                return fw[part][:, n, :], src[:, :]
            if n < DC + DC // 2:
                c = 2 * (n - DC)
                return (ar[part][:, c:c + 2, 0:ER + NR],
                        src[:, :].rearrange("p (c n) -> p c n", c=2)[:, :, 0:ER + NR])
            return bt[part], src[:, :]

        @block.sync
        def _(sp):
            def load_qk(h):
                sp.dma_start(wq_raw[:, :, :], wq_d[:, :, bass.ds(h * DH, DH)]).then_inc(ld_wq, 16)

            def load_k(h):
                sp.dma_start(wk_raw[:, :, :], wk_d[:, :, bass.ds(h * DH, DH)]).then_inc(ld_wk, 16)

            def load_bias(h):
                for f in range(2):
                    for i in range(2):
                        sp.dma_start(bias[64 * f:64 * f + 64, i::2, :],
                                     bias_d[f, i, bass.ds(h, 1)].rearrange("o q j k -> (o q) j k")
                                     ).then_inc(ld_bias, 16)

            def load_wo(pair):
                sp.dma_start(wo_raw[:, :, :], wo_d[:, bass.ds(2 * pair, 2), :]).then_inc(ld_wo, 16)

            for t in range(NT):
                sp.dma_start(v[:, t, :], ctx_d[:, t, :]).then_inc(ld_ctx[t], 16)
                if t == 0:
                    for c in range(DC):
                        sp.dma_start(bw_raw[:, c, :], wv_d[c, :, 0:GD]).then_inc(ld_wv0[c], 16)
            load_qk(0)
            load_k(0)
            for f in range(2):
                for i in range(2):
                    sp.dma_start(mask8[64 * f:64 * f + 64, i::2, :], mask_d[f, i]).then_inc(ld_mask, 16)
            load_bias(0)
            load_wo(0)
            sp.dma_start(bb[:, :], base_b.partition_broadcast(P)).then_inc(ld_small, 16)
            sp.dma_start(rb[:, :], router_b.partition_broadcast(P)).then_inc(ld_small, 16)
            sp.dma_start(mapi[:, :], emap.partition_broadcast(P)).then_inc(ld_small, 16)
            for h in (1, 2):
                sp.wait_ge(wq_l, h)
                load_qk(h)
                sp.wait_ge(wk_l, h)
                load_k(h)

            def group(g, last=False):
                for s in range(GH):
                    h = g * GH + s
                    if not last:
                        sp.wait_ge(wv_l, g * GH + (s + GH))
                        sp.dma_start(wv_raw[:, :], wv_d[s, :, bass.ds((g + 1) * GD, GD)]).then_inc(ld_wv, 16)
                    if has_next(last, s, 1):
                        sp.wait_ge(s_read, h + 1)
                        load_bias(h + 1)
                    if has_next(last, s, 3):
                        sp.wait_ge(wq_l, h + 3)
                        load_qk(h + 3)
                    if s % 2 and has_next(last, s, 1):
                        pair = g * 2 + s // 2
                        sp.wait_ge(wo_l, pair + 1)
                        load_wo(pair + 1)
                    if has_next(last, s, 3):
                        sp.wait_ge(wk_l, h + 3)
                        load_k(h + 3)
                    if last and s == 0:
                        sp.dma_start(bw_raw[:, :, :], bw_d).then_inc(ld_ffn, 16)
                        sp.dma_start(a_raw[:, :], a_d).then_inc(ld_ffn, 16)
                        sp.dma_start(r_raw[:, :], router_W).then_inc(ld_ffn, 16)
                        for o in range(DC):
                            sp.dma_start(b_raw[:, o, :].rearrange("p (e r) -> p e r", e=E),
                                         b_d[:, o]).then_inc(ld_ffn, 16)

            group(0)
            with sp.Fori(1, G - 1) as g:
                group(g)
            group(G - 1, last=True)
            for t in range(NT):
                sp.wait_ge(out_made, t + 1)
                sp.dma_start(out_d[:, t, :], y[:, t, :]).then_inc(stored, 16)
            sp.wait_ge(stored, 16 * NT)

        @block.gpsimd
        def _(pool):
            nc.gpsimd.memset(ident[:, :], 0.0).then_inc(made0, 1)
            pool.wait_ge(made0, 1)
            nc.gpsimd.affine_select(out=ident[:, :], in_=ident[:, :], compare_op=ALU.not_equal, fill=1.0,
                                    base=0, pattern=[[-1, P]], channel_multiplier=1).then_inc(made, 1)
            nc.gpsimd.memset(mhalf[:, :], -0.5).then_inc(made0, 1)
            pool.wait_ge(made0, 2)

            def rstd_of(n):
                pool.wait_ge(ve_made, n + 1)
                nc.gpsimd.tensor_tensor(rstd[:, n % 2:n % 2 + 1], ve[:, n % 2:n % 2 + 1], mhalf[:, :],
                                        ALU.pow).then_inc(rstd_made, 1)

            rstd_of(0)
            nc.gpsimd.memset(pT[:, :, :], 0.0).then_inc(made, 1)
            for t in range(1, NT):
                rstd_of(t)

            def add_mask(h):
                pool.wait_ge(ld_bias, (h + 1) * 64)
                nc.gpsimd.tensor_tensor(bias[:, :, :], bias[:, :, :], madd[:, :, :], ALU.add).then_inc(bias_made, 1)

            pool.wait_ge(mask_made, 1)
            for s in range(GH):
                add_mask(s)
            with pool.Fori(1, G) as g:
                for s in range(GH):
                    add_mask(g * GH + s)
            pool.wait_ge(ld_small, 48)
            for t in range(NT):
                rstd_of(NT + t)
                pool.wait_ge(xn_made, NT + t + 1)
                nc.gpsimd.tensor_tensor(y[:, t, :], y[:, t, :], bb[:, :], ALU.add).then_inc(yb_made, 1)

        @block.scalar
        def _(act):
            for t in range(NT):
                act.dma_start(y[:, t, :], x_d[:, t, :]).then_inc(ld_x[t], 16)
            act.wait_ge(made0, 2)
            nc.scalar.activation(warm[:, :], mhalf[:, :], ACT.Exp).then_inc(warmed, 1)

            def copy_out(e, dst, src):
                act.wait_ge(proj_full, e + 1)
                nc.scalar.copy(dst, src).then_inc(proj_free, 1)

            def split_q(h):
                act.wait_ge(ld_wq, (h + 1) * 16)
                nc.scalar.copy(wq_hi[:, :, :], wq_raw[:, :, :]).then_inc(wq_h, 1)

            def split_k(h):
                act.wait_ge(ld_wk, (h + 1) * 16)
                nc.scalar.copy(wk_hi[:, :, :], wk_raw[:, :, :]).then_inc(wk_h, 1)

            def project_out(base, half, dst):
                e = base + half
                copy_out(e, dst[:, half % 2 * HALF:half % 2 * HALF + HALF], pP[half % 2][:, :])

            for step in OPENING:
                kind, i = step
                if step in PROJECTED:
                    e = PROJECTED.index(step)
                    cols = slice(i * HALF, (i + 1) * HALF)
                    dst = v[:, i, :] if kind == "v" else (qT if kind == "q" else kT)[:, cols]
                    copy_out(e, dst, pP[e % 2][:, :])
                    if step == ("k", 1):
                        split_k(1)
                    if step == ("q", 1):
                        split_q(1)
                    continue
                n, src = turn_of(step)
                dst = xT_hi if kind == "x" else cTh
                act.wait_ge(turned, n + 1)
                nc.scalar.copy(dst[:, :, i * P:(i + 1) * P], src[:, :].rearrange("p (c t) -> p c t", c=DC)
                               ).then_inc(turned_hi, 1)
                if step == ("ctx", 0):
                    for c in range(DC):
                        act.wait_ge(ld_wv0[c], 16)
                        nc.scalar.copy(wv_hi[:, c, :], bw_raw[:, c, :]).then_inc(wv_h, 1)
                if step == ("ctx", 4):
                    split_q(0)
                if step == ("ctx", 6):
                    split_k(0)

            def split_ffn(n):
                act.wait_ge(fw_full, n + 1)
                dst, src = ffn_weight(n, 0)
                if n == NFW - 1:
                    nc.scalar.mul(dst, src, LORA_SCALE).then_inc(fw_hi, 1)
                else:
                    nc.scalar.copy(dst, src).then_inc(fw_hi, 1)

            def group(g, last=False):
                for s in range(GH):
                    h = g * GH + s
                    base = g * PG + (P0 + 2 * NH * s)
                    act.wait_ge(sub_made, h + 1)
                    nc.scalar.activation(pr[:, :, :], sc[:, :, :], ACT.Exp).then_inc(exp_made, 1)
                    if has_next(last, s, 1):
                        project_out(base, 0, qT)
                        project_out(base, 1, qT)
                    act.wait_ge(t_full, h + 1)
                    nc.scalar.copy(pT[0:64, :, 0:64], pT_[0:64, :].rearrange("p (j q) -> p j q", q=64)
                                   ).then_inc(t_lower, 1)
                    if has_next(last, s, 2):
                        split_q(h + 2)
                    if not last:
                        act.wait_ge(ld_wv, g * 64 + 16 * (s + 1))
                        nc.scalar.copy(wv_hi[:, s, :], wv_raw[:, :]).then_inc(wv_h, 1)
                    if s % 2 and has_next(last, s, 1):
                        act.wait_ge(ld_wo, g * 32 + 16 * (s // 2 + 1))
                        nc.scalar.copy(wo_hi[:, :, :], wo_raw[:, :, :]).then_inc(wo_h, 1)
                    if has_next(last, s, 1):
                        project_out(base, 2, kT)
                        project_out(base, 3, kT)
                    if has_next(last, s, 2):
                        split_k(h + 2)
                    if last and s == 1:
                        for n in range(DC):
                            split_ffn(n)
                    if last and s == 2:
                        act.wait_ge(ld_wo, 16 * (H // 2))
                        for i in range(2):
                            ins = nc.scalar.copy(last_wo[0][i], wo_raw[:, i, :])
                        ins.then_inc(wo_h, 1)
                    if last and s == 3:
                        for n in range(DC, NFW):
                            split_ffn(n)
                    hi = last_oT[0] if last and s >= 2 else oT_hi
                    for i in range(NH):
                        act.wait_ge(o_full, h * 2 + (i + 1))
                        nc.scalar.copy(hi[:, s % 2, i * HALF:(i + 1) * HALF], pO[i][:, :]).then_inc(o_hi, 1)
                    if s == GH - 1 and not last:
                        for t in range(NT):
                            copy_out(g * PG + (P0 + GH * 2 * NH + t), v[:, t, :], pP[t % 2][:, :])

            group(0)
            with act.Fori(1, G - 1) as g:
                group(g)
            group(G - 1, last=True)

            for t in range(NT):
                act.wait_ge(turned, 2 * NT + t + 1)
                nc.scalar.copy(xT_hi[:, :, t * P:(t + 1) * P],
                               pTurn[t % 2][:, :].rearrange("p (c t) -> p c t", c=DC)).then_inc(turned_hi, 1)
            for k in range(NT // NRB):
                act.wait_ge(lg_made, k + 1)
                tiles = slice(k * NRB, (k + 1) * NRB)
                nc.scalar.activation(ex[:, tiles, :], lg[:, tiles, :], ACT.Exp).then_inc(ex_made, 1)
            for t in range(NT):
                act.wait_ge(hwT_full, t + 1)
                nc.scalar.copy(hwT_hi[:, t % 2, :], pTurn[t % 2][:, 0:P]).then_inc(hwT_h, 1)

        @block.vector
        def _(dve):
            def lower(dst, src, hi, done):
                nc.vector.tensor_tensor(dst, src, hi.bitcast(F32), ALU.subtract).then_inc(done, 1)

            def split_q(h):
                dve.wait_ge(wq_h, h + 1)
                lower(wq_lo[:, :, :], wq_raw[:, :, :], wq_hi[:, :, :], wq_l)

            def split_k(h):
                dve.wait_ge(wk_h, h + 1)
                lower(wk_lo[:, :, :], wk_raw[:, :, :], wk_hi[:, :, :], wk_l)

            def stats(n, t):
                b = n % 2
                nc.vector.bn_stats(st[:, b, :], y[:, t, :]).then_inc(ln_step, 1)
                dve.wait_ge(ln_step, 2 * n + 1)
                nc.vector.bn_aggr(mv[:, b, :], st[:, b, :]).then_inc(ln_step, 1)
                dve.wait_ge(ln_step, 2 * n + 2)
                nc.vector.tensor_scalar(ve[:, b:b + 1], mv[:, b, 1:2], EPS, None, ALU.add).then_inc(ve_made, 1)

            def normalise(n, t):
                b = n % 2
                dve.wait_ge(rstd_made, n + 1)
                if n >= 2:
                    dve.wait_ge(turned, turned_before(n))
                nc.vector.tensor_scalar(xn[:, b, :], y[:, t, :], mv[:, b, 0:1], rstd[:, b:b + 1],
                                        ALU.subtract, ALU.mult).then_inc(xn_made, 1)

            def turned_before(n):
                m = n - 2
                return (TURNED.index(("x", m)) if m < NT else NT + m) + 1

            def prepare(t):
                dve.wait_ge(ld_x[t], 16)
                stats(t, t)

            for step in OPENING:
                kind, i = step
                if step in PROJECTED:
                    if kind == "v":
                        if i + 2 < NT:
                            prepare(i + 2)
                        if i + 1 < NT:
                            normalise(i + 1, i + 1)
                    continue
                n, src = turn_of(step)
                hi, lo = (xT_hi, xT_lo) if kind == "x" else (cTh, cTl)
                dve.wait_ge(turned_hi, n + 1)
                lower(lo[:, :, i * P:(i + 1) * P], src[:, :].rearrange("p (c t) -> p c t", c=DC),
                      hi[:, :, i * P:(i + 1) * P], turned_lo)
                if step == ("ctx", 0):
                    for c in range(DC):
                        dve.wait_ge(wv_h, c + 1)
                        lower(wv_lo[:, c, :], bw_raw[:, c, :], wv_hi[:, c, :], wv_l)
                    prepare(0)
                    prepare(1)
                    normalise(0, 0)
                if step == ("ctx", 4):
                    split_q(0)
                if step == ("ctx", 6):
                    split_k(0)
            dve.wait_ge(ld_mask, 64)
            nc.vector.tensor_scalar(madd[:, :, :], mask8[:, :, :], -NEG, NEG, ALU.mult, ALU.add).then_inc(mask_made, 1)
            nc.vector.tensor_reduce(some[:, :], mask8[:, :, :], AX.X, ALU.max).then_inc(msk, 1)
            dve.wait_ge(ld_small, 48)
            nc.vector.tensor_copy(mapf[:, :], mapi[:, :]).then_inc(msk, 1)
            dve.wait_ge(msk, 2)
            for e in range(E):
                nc.vector.tensor_scalar(onehot[:, e, :], mapf[:, :], float(e), None, ALU.is_equal).then_inc(sel_made, 1)
            split_k(1)
            split_q(1)

            def split_ffn(n):
                dve.wait_ge(fw_hi, n + 1)
                dst, src = ffn_weight(n, 1)
                hi, _ = ffn_weight(n, 0)
                if n == NFW - 1:
                    nc.vector.scalar_tensor_tensor(out=dst, in0=src, scalar=LORA_SCALE, in1=hi.bitcast(F32),
                                                   op0=ALU.mult, op1=ALU.subtract).then_inc(fw_lo, 1)
                else:
                    lower(dst, src, hi, fw_lo)

            def add_tile(pair, t):
                dve.wait_ge(y_full, pair * NT + (t + 1))
                nc.vector.tensor_tensor(y[:, t, :], y[:, t, :], pY[t % 2][:, :], ALU.add).then_inc(y_added, 1)

            last_pair = H // 2 - 1

            def group(g, first=False, last=False):
                for s in range(GH):
                    h = g * GH + s
                    step = h * 4
                    dve.wait_ge(s_full, h + 1)
                    dve.wait_ge(bias_made, h + 1)
                    nc.vector.scalar_tensor_tensor(out=sc[:, :, :], in0=pS[:, :].rearrange("p (b k) -> p b k", k=S),
                                                   scalar=SCALE, in1=bias[:, :, :], op0=ALU.mult,
                                                   op1=ALU.add).then_inc(s_read, 1)
                    dve.wait_ge(s_read, h + 1)
                    nc.vector.tensor_reduce(mx[:, :], sc[:, :, :], AX.X, ALU.max).then_inc(sm_step, 1)
                    dve.wait_ge(sm_step, step + 1)
                    nc.vector.tensor_tensor(sc[:, :, :], sc[:, :, :],
                                            mx[:, :].unsqueeze(2).to_broadcast([P, NB, S]),
                                            ALU.subtract).then_inc(sub_made, 1)
                    if last and s == 3:
                        for t in (4, 5):
                            add_tile(last_pair - 1, t)
                    dve.wait_ge(exp_made, h + 1)
                    nc.vector.tensor_reduce(sm[:, :], pr[:, :, :], AX.X, ALU.add).then_inc(sm_step, 1)
                    dve.wait_ge(sm_step, step + 2)
                    nc.vector.reciprocal(rs[:, :], sm[:, :]).then_inc(sm_step, 1)
                    dve.wait_ge(sm_step, step + 3)
                    nc.vector.tensor_tensor(rs[:, :], rs[:, :], some[:, :], ALU.mult).then_inc(sm_step, 1)
                    dve.wait_ge(sm_step, step + 4)
                    nc.vector.tensor_tensor(pr[:, :, :], pr[:, :, :],
                                            rs[:, :].unsqueeze(2).to_broadcast([P, NB, S]),
                                            ALU.mult).then_inc(p_made, 1)
                    if last and s == 3:
                        for t in (6, 7):
                            add_tile(last_pair - 1, t)
                    dve.wait_ge(t_full, h + 1)
                    nc.vector.tensor_copy(pT[64:128, :, 64:128], pT_[64:128, :].rearrange("p (j q) -> p j q", q=64)
                                          ).then_inc(t_upper, 1)
                    if has_next(last, s, 2):
                        split_q(h + 2)
                    if not last:
                        dve.wait_ge(wv_h, g * GH + (GH + s + 1))
                        lower(wv_lo[:, s, :], wv_raw[:, :], wv_hi[:, s, :], wv_l)
                    if s % 2 and has_next(last, s, 1):
                        dve.wait_ge(wo_h, g * 2 + (s // 2 + 1))
                        lower(wo_lo[:, :, :], wo_raw[:, :, :], wo_hi[:, :, :], wo_l)
                    if has_next(last, s, 2):
                        split_k(h + 2)
                    if s % 2 == 0 and not (first and s == 0):
                        for t in range(4 if last and s == 2 else NT):
                            add_tile(g * 2 + (s // 2 - 1), t)
                    if last and s == 1:
                        for n in range(DC):
                            split_ffn(n)
                    if last and s == 2:
                        dve.wait_ge(wo_h, last_pair + 1)
                        for i in range(2):
                            ins = nc.vector.tensor_tensor(last_wo[1][i], wo_raw[:, i, :], last_wo[0][i].bitcast(F32),
                                                          ALU.subtract)
                        ins.then_inc(wo_l, 1)
                    if last and s == 3:
                        for n in range(DC, NFW):
                            split_ffn(n)
                    hi, lo = last_oT if last and s >= 2 else (oT_hi, oT_lo)
                    for i in range(NH):
                        cols = slice(i * HALF, (i + 1) * HALF)
                        dve.wait_ge(o_hi, h * 2 + (i + 1))
                        lower(lo[:, s % 2, cols], pO[i][:, :], hi[:, s % 2, cols], o_lo)

            group(0, first=True)
            with dve.Fori(1, G - 1) as g:
                group(g)
            group(G - 1, last=True)

            dve.wait_ge(sel_made, E)
            for part in range(2):
                ins = nc.vector.memset(ar[part][:, :, ER + NR:ARW].bitcast(U32), 0)
            ins.then_inc(sel_made, 1)

            def chain(ins, n):
                ins.then_inc(r_step, 1)
                dve.wait_ge(r_step, n + 1)

            def two(bank_):
                return bank_[:, :].rearrange("p (t n) -> p t n", t=2)

            def route(k):
                n = k * RB
                tiles = slice(k * NRB, (k + 1) * NRB)
                dve.wait_ge(g_full, (k + 1) * NRB)
                for i in (2 * k, 2 * k + 1):
                    ins = nc.vector.tensor_tensor(lg[:, 2 * i:2 * i + 2, :], two(pG[i])[:, :, ER:ER + NR],
                                                  rb[:, :].unsqueeze(1).to_broadcast([P, 2, NR]), ALU.add)
                    chain(ins, n + i - 2 * k)
                chain(nc.vector.tensor_reduce(lmax[:, tiles], lg[:, tiles, :], AX.X, ALU.max), n + 2)
                nc.vector.tensor_tensor(lg[:, tiles, :], lg[:, tiles, :],
                                        lmax[:, tiles].unsqueeze(2).to_broadcast([P, NRB, NR]), ALU.subtract
                                        ).then_inc(lg_made, 1)
                dve.wait_ge(ex_made, k + 1)
                chain(nc.vector.tensor_reduce(esum[:, tiles], ex[:, tiles, :], AX.X, ALU.add), n + 3)
                for t in range(k * NRB, (k + 1) * NRB):
                    ins = nc.vector.max(top[:, t, :], ex[:, t, :])
                chain(ins, n + 4)
                nc.vector.reciprocal(rsum[:, tiles], esum[:, tiles]).then_inc(r_step, 1)
                for t in range(k * NRB, (k + 1) * NRB):
                    ins = nc.vector.match_replace(left[:, t, :], top[:, t, :], ex[:, t, :], -1.0)
                chain(ins, n + 6)
                chain(nc.vector.scalar_tensor_tensor(out=kept[:, tiles, :], in0=left[:, tiles, :], scalar=0.0,
                                                     in1=ex[:, tiles, :], op0=ALU.is_lt, op1=ALU.mult), n + 7)
                chain(nc.vector.tensor_tensor(ew[:, :, :, :], onehot[:, :, :].unsqueeze(1).to_broadcast([P, NRB, E, NR]),
                                              kept[:, tiles, :].unsqueeze(2).to_broadcast([P, NRB, E, NR]),
                                              ALU.mult), n + 8)
                chain(nc.vector.tensor_reduce(we[:, tiles, :], ew[:, :, :, :], AX.X, ALU.add), n + 9)
                chain(nc.vector.tensor_tensor(wn[:, tiles, :], we[:, tiles, :],
                                              rsum[:, tiles].unsqueeze(2).to_broadcast([P, NRB, E]), ALU.mult), n + 10)
                for t in range(k * NRB, (k + 1) * NRB):
                    nc.vector.tensor_tensor(hw[:, t, :].rearrange("p (e r) -> p e r", e=E),
                                            two(pG[t // 2])[:, t % 2, 0:ER].rearrange("p (e r) -> p e r", e=E),
                                            wn[:, t, :].unsqueeze(2).to_broadcast([P, E, R]), ALU.mult
                                            ).then_inc(hw_made, 1)

            for t in range(NT + 2):
                if t < NT:
                    add_tile(last_pair, t)
                    dve.wait_ge(y_added, last_pair * NT + t + 1)
                    stats(NT + t, t)
                if 1 <= t <= NT:
                    normalise(NT + t - 1, t - 1)
                if t >= 2:
                    dve.wait_ge(turned_hi, 2 * NT + t - 1)
                    cols = slice((t - 2) * P, (t - 1) * P)
                    lower(xT_lo[:, :, cols], pTurn[t % 2][:, :].rearrange("p (c t) -> p c t", c=DC),
                          xT_hi[:, :, cols], turned_lo)
            for k in range(NT // NRB):
                route(k)
            for t in range(NT + 1):
                if t < NT:
                    dve.wait_ge(hwT_h, t + 1)
                    lower(hwT_lo[:, t % 2, :], pTurn[t % 2][:, 0:P], hwT_hi[:, t % 2, :], hwT_l)
                if t >= 1:
                    dve.wait_ge(f_full, t)
                    dve.wait_ge(yb_made, t)
                    nc.vector.tensor_tensor(y[:, t - 1, :], y[:, t - 1, :], pF[(t - 1) % 3][:, :], ALU.add
                                            ).then_inc(out_made, 1)

        @block.tensor
        def _(pe):
            def product(bank_, pairs, first=True, last=True):
                terms = [(a[i], b[j]) for a, b in pairs for i, j in ((0, 0), (1, 0), (0, 1))]
                for n, (a, b) in enumerate(terms):
                    mm = nc.tensor.matmul(bank_, a, b, start=first and n == 0, stop=last and n == len(terms) - 1)
                return mm

            def bank_free(e):
                if not isinstance(e, int) or e >= 2:
                    pe.wait_ge(proj_free, e - 1)

            def project(e, n, w, xt, half):
                bank_free(e)
                cols = slice(half * HALF, (half + 1) * HALF)
                product(pP[n][:, :], [((w[0][:, c, :], w[1][:, c, :]), (xt[0][:, c, cols], xt[1][:, c, cols]))
                                      for c in range(DC)]).then_inc(proj_full, 1)

            def v_tile(e, n, t, opening=False):
                bank_free(e)
                cols = slice(t * P, (t + 1) * P)
                for c in range(DC):
                    if opening:
                        pe.wait_ge(wv_l, c + 1)
                    mm = product(pP[n][:, :], [((cTh[:, c, cols], cTl[:, c, cols]), (wv_hi[:, c, :], wv_lo[:, c, :]))],
                                 first=c == 0, last=c == DC - 1)
                mm.then_inc(proj_full, 1)

            def turn(n, src, dst):
                for c in range(DC):
                    mm = nc.tensor.transpose(dst[:, c * P:(c + 1) * P], src[:, c * P:(c + 1) * P], ident[:, :])
                mm.then_inc(turned, 1)

            WQ, WK = (wq_hi, wq_lo), (wk_hi, wk_lo)
            XT, CT = (xT_hi, xT_lo), (cTh, cTl)

            pe.wait_ge(made, 1)
            for step in OPENING:
                kind, i = step
                if kind == "v":
                    pe.wait_ge(turned_lo, TURNED.index(("ctx", i)) + 1)
                    e = PROJECTED.index(step)
                    v_tile(e, e % 2, i, opening=i == 0)
                    continue
                if kind in ("q", "k"):
                    tile = ("x" if kind == "q" else "ctx", (i + 1) * (NT // 2) - 1)
                    pe.wait_ge(turned_lo, TURNED.index(tile) + 1)
                    pe.wait_ge(wq_l if kind == "q" else wk_l, 1)
                    e = PROJECTED.index(step)
                    project(e, e % 2, *((WQ, XT) if kind == "q" else (WK, CT)), i)
                    continue
                n, dst = turn_of(step)
                if i >= 2:
                    pe.wait_ge(turned_lo, TURNED.index((kind, i - 2)) + 1)
                if kind == "ctx":
                    pe.wait_ge(ld_ctx[i], 16)
                    turn(n, v[:, i, :], dst)
                else:
                    pe.wait_ge(xn_made, i + 1)
                    turn(n, xn[:, i % 2, :], dst)

            last_pair = H // 2 - 1

            def wo_terms(pair, t, i):
                cols = slice(t * P, (t + 1) * P)
                if isinstance(pair, int) and pair == last_pair:
                    return ([o[:, i, cols] for o in last_oT], [w[i] for w in last_wo])
                return ((oT_hi[:, i, cols], oT_lo[:, i, cols]), (wo_hi[:, i, :], wo_lo[:, i, :]))

            def times_wo(pair, t, heads=(0, 1)):
                mm = product(pY[t % 2][:, :], [wo_terms(pair, t, i) for i in heads],
                             first=heads[0] == 0, last=heads[-1] == 1)
                if heads[-1] == 1:
                    mm.then_inc(y_full, 1)

            def pair_times_wo(pair, tiles, free_at_first=False):
                for t in tiles:
                    if not (free_at_first and t < 2):
                        pe.wait_ge(y_added, pair * NT + (t - 1))
                    times_wo(pair, t)

            def group(g, first=False, last=False):
                for s in range(GH):
                    h = g * GH + s
                    base = g * PG + (P0 + 2 * NH * s)
                    if s == 0:
                        pe.wait_ge(proj_free, P0 - 1 if first else g * PG + (P0 - NT))
                    else:
                        pe.wait_ge(proj_free, base)
                    for half in range(2):
                        for b in [b for b in range(B) if b // 2 % 2 == half]:
                            blk = 2 * (b // 4) + b % 2
                            mm = nc.tensor.matmul(pS[64 * half:64 * half + 64, blk * S:(blk + 1) * S],
                                                  qT[:, b * S:(b + 1) * S], kT[:, b * S:(b + 1) * S],
                                                  start=True, stop=True)
                    mm.then_inc(s_full, 1)
                    if has_next(last, s, 1):
                        pe.wait_ge(wq_l, h + 2)
                        for half in range(NH):
                            project(base + half, half, WQ, XT, half)
                    elif last:
                        pair_times_wo(last_pair - 1, range(4, NT))
                    pe.wait_ge(p_made, h + 1)
                    for j in range(NB // 2):
                        mm = nc.tensor.transpose(pT_[:, j * P:(j + 1) * P],
                                                 pr[:, 2 * j:2 * j + 2, :].rearrange("p a k -> p (a k)"), ident[:, :])
                    mm.then_inc(t_full, 1)
                    if has_next(last, s, 1):
                        pe.wait_ge(wk_l, h + 2)
                        for half in range(NH):
                            project(base + (NH + half), half, WK, CT, half)
                    if s % 2 == 0 and not (first and s == 0):
                        pair = g * 2 + (s // 2 - 1)
                        pe.wait_ge(wo_l, pair + 1)
                        pe.wait_ge(o_lo, h * 2)
                        pair_times_wo(pair, range(4 if last and s == 2 else NT), first and s == 2)
                    if last and s == 1:
                        pe.wait_ge(y_added, (last_pair - 1) * NT)
                        ffn_weights(0, DC)
                    if last and s == 3:
                        ffn_weights(DC, NFW)
                    pe.wait_ge(t_lower, h + 1)
                    pe.wait_ge(t_upper, h + 1)
                    if not (first and s == 0):
                        pe.wait_ge(o_lo, h * 2)
                    if s == 0:
                        pe.wait_ge(proj_free, g * PG + P0)
                        if first:
                            pe.wait_ge(made, 2)
                    for i in range(NH):
                        for q in range(NT // 2):
                            t = i * (NT // 2) + q
                            mm = nc.tensor.matmul(pO[i][:, q * P:(q + 1) * P], v[:, t, s * DH:(s + 1) * DH],
                                                  pT[:, t, :], start=True, stop=True)
                        mm.then_inc(o_full, 1)
                    if s == GH - 1 and not last:
                        pe.wait_ge(wv_l, g * GH + 2 * GH)
                        for t in range(NT):
                            v_tile(g * PG + (P0 + GH * 2 * NH + t), t % 2, t)

            def ffn_weights(begin, end):
                pe.wait_ge(ld_ffn, 16 * (3 + DC))
                for n in range(begin, end):
                    dst = (pY if n < DC else pP)[n % 2]
                    if n >= begin + 2:
                        pe.wait_ge(fw_lo, n - 1)
                    elif n >= DC:
                        pe.wait_ge(proj_free, P0 + (G - 1) * PG + 3 * 2 * NH)
                    if n < DC:
                        for o in range(DC):
                            mm = nc.tensor.transpose(dst[:, o * P:(o + 1) * P], bw_raw[:, o, n * P:(n + 1) * P],
                                                     ident[:, :])
                    elif n < NFW - 1:
                        for i in range(2):
                            c = 2 * (n - DC) + i
                            nc.tensor.transpose(dst[:, i * ARW:i * ARW + ER], a_raw[:, c * P:(c + 1) * P],
                                                ident[:, :])
                            mm = nc.tensor.transpose(dst[:, i * ARW + ER:i * ARW + ER + NR],
                                                     r_raw[:, c * P:(c + 1) * P], ident[0:NR, 0:NR])
                    else:
                        for o in range(DC):
                            mm = nc.tensor.transpose(dst[:, o * P:(o + 1) * P], b_raw[:, o, :], ident[:, :])
                    mm.then_inc(fw_full, 1)

            group(0, first=True)
            with pe.Fori(1, G - 1) as g:
                group(g)
            group(G - 1, last=True)

            def turn_last(t):
                pe.wait_ge(xn_made, NT + t + 1)
                if t >= 2:
                    pe.wait_ge(turned_lo, 2 * NT + t - 1)
                turn(2 * NT + t, xn[:, t % 2, :], pTurn[t % 2])

            def xt_parts(t):
                cols = slice(t * P, (t + 1) * P)
                return [(xT_hi[:, c, cols], xT_lo[:, c, cols]) for c in range(DC)]

            def h_and_logits(t):
                pe.wait_ge(turned_lo, 2 * NT + t + 1)
                if t == 0:
                    pe.wait_ge(fw_lo, NFW)
                    pe.wait_ge(sel_made, E + 1)
                product(pG[t // 2][:, t % 2 * ARW:(t % 2 + 1) * ARW],
                        [(xt, (ar[0][:, c, :], ar[1][:, c, :])) for c, xt in enumerate(xt_parts(t))]
                        ).then_inc(g_full, 1)

            def base(t):
                if t >= 3:
                    pe.wait_ge(out_made, t - 2)
                product(pF[t % 3][:, :], [(xt, (fw[0][:, c, :], fw[1][:, c, :])) for c, xt in enumerate(xt_parts(t))],
                        last=False)

            def turn_hw(t):
                pe.wait_ge(hw_made, t + 1)
                if t >= 2:
                    pe.wait_ge(hwT_l, t - 1)
                nc.tensor.transpose(pTurn[t % 2][:, 0:P], hw[:, t, :], ident[:, :]).then_inc(hwT_full, 1)

            def lora(t):
                pe.wait_ge(hwT_l, t + 1)
                product(pF[t % 3][:, :], [((hwT_hi[:, t % 2, :], hwT_lo[:, t % 2, :]), bt)], first=False
                        ).then_inc(f_full, 1)

            for t in range(2):
                pe.wait_ge(y_added, last_pair * NT + t - 1)
                if t == 0:
                    pe.wait_ge(wo_l, last_pair + 1)
                times_wo(last_pair, t, heads=(0,))
            pe.wait_ge(o_lo, 2 * H)
            for t in range(2):
                times_wo(last_pair, t, heads=(1,))
            for i in range(2, NT + 5):
                if i < NT:
                    pair_times_wo(last_pair, (i,))
                if 3 <= i < NT + 3:
                    turn_last(i - 3)
                if i >= 5:
                    if i == NT + 1:
                        pe.wait_ge(y_added, (last_pair + 1) * NT)
                    h_and_logits(i - 5)
            base(0)
            for t in range(NT):
                if t + 1 < NT:
                    base(t + 1)
                for i in ((0, 1) if t == 0 else (t + 1,)):
                    if i < NT:
                        turn_hw(i)
                lora(t)


_INS = ["x", "ctx_4096", "fside_Bx32xSxS2_0", "mask_BxSxS2_bk0", "L0_xattn_Wq", "L0_xattn_Wk", "L0_xattn_Wv",
        "L0_xattn_Wo", "L0_ffn_base_W", "L0_ffn_base_b", "L0_ffn_router_W", "L0_ffn_router_b", "L0_ffn_A",
        "L0_ffn_B", "L0_ffn_expert_map"]


def kernel(**inputs):
    import numpy as _np
    import concourse.bacc as _bacc
    from concourse import mybir as _mybir
    from concourse.bass_utils import run_bass_kernel_spmd as _run

    nc = _bacc.Bacc("TRN2", target_bir_lowering=False, num_devices=1)
    arrays, args = {}, []
    for name in _INS:
        a = _np.ascontiguousarray(inputs[name])
        arrays[f"in_{name}"] = a
        args.append(nc.dram_tensor(f"in_{name}", a.shape, _mybir.dt.from_np(a.dtype), kind="ExternalInput").ap())
    out = nc.dram_tensor("out_0", (B, S, D), _mybir.dt.float32, kind="ExternalOutput").ap()
    xattn_ffn(nc, *args, out)
    r = _run(nc, [arrays], core_ids=[0])
    return r.results[0]["out_0"]
```

```python
from contextlib import ExitStack

import concourse.bass as bass
from concourse import mybir

F32 = mybir.dt.float32
F32R = mybir.dt.float32r
U32 = mybir.dt.uint32
U8 = mybir.dt.uint8
I32 = mybir.dt.int32
ALU = mybir.AluOpType
ACT = mybir.ActivationFunctionType
AX = mybir.AxisListType

P = 128
B, S, D, H, DH = 16, 64, 512, 32, 128
T = B * S
NT = T // P
DC = D // P
HALF = T // 2
NH = T // HALF
GH = 4
G = H // GH
GD = GH * DH
NB = B // 2
E, R, NR = 8, 16, 15
ER = E * R
ARW = 256
SCALE = float(DH) ** -0.5
LORA_SCALE = 2.0
EPS = 1e-5
NEG = -1e30

OPENING = []
for i in range(NT + 2):
    if i < NT:
        OPENING.append(("ctx", i))
    if i >= 2:
        OPENING.append(("x", i - 2))
    if 1 <= i < NT:
        OPENING.append(("v", i - 1))
OPENING += [("k", 0), ("k", 1), ("q", 0), ("q", 1), ("v", NT - 1)]
TURNED = [step for step in OPENING if step[0] in ("ctx", "x")]
PROJECTED = [step for step in OPENING if step not in TURNED]
P0 = len(PROJECTED)
PG = GH * 2 * NH + NT
NFW = DC + DC // 2 + 1
NX = 4
NRB = NT // 2
RB = 11


def xattn_ffn(nc, x, ctx_in, bias_in, mask_in, Wq, Wk, Wv, Wo, base_W, base_b, router_W, router_b,
              A_in, B_in, emap, out):
    x_d = x.rearrange("(a c) s d -> (c s) a d", c=2)
    ctx_d = ctx_in.rearrange("(a c) s d -> (c s) a d", c=2)
    out_d = out.rearrange("(a c) s d -> (c s) a d", c=2)
    wq_d = Wq.rearrange("(c p) n -> p c n", p=P)
    wk_d = Wk.rearrange("(c p) n -> p c n", p=P)
    wv_d = Wv.rearrange("(c p) n -> c p n", p=P)
    wo_d = Wo.rearrange("(h p) n -> p h n", p=P)
    bw_d = base_W.rearrange("(o p) d -> p o d", p=P)
    a_d = A_in.rearrange("e r d -> (e r) d")
    b_d = B_in.rearrange("e (o p) r -> p o e r", p=P)
    bias_d = bias_in.rearrange("(j f i) h q k -> f i h q j k", f=2, i=2)
    mask_d = mask_in.rearrange("(j f i) q k -> f i q j k", f=2, i=2)

    with ExitStack() as stack:
        def sb(name, shape, dt=F32):
            return stack.enter_context(nc.sbuf_tensor(name, shape, dt))

        def bank(name):
            return stack.enter_context(nc.psum_tensor(name, [P, 512], F32))

        def sem(name):
            return stack.enter_context(nc.semaphore(name))

        xT_hi = sb("xT_hi", [P, DC, T], F32R)
        xT_lo = sb("xT_lo", [P, DC, T], F32R)
        cT_hi = sb("cT_hi", [P, DC * T], F32R)
        cT_lo = sb("cT_lo", [P, DC * T], F32R)
        wq_hi = sb("wq_hi", [P, DC, DH], F32R)
        wq_lo = sb("wq_lo", [P, DC, DH], F32R)
        wk_hi = sb("wk_hi", [P, DC, DH], F32R)
        wk_lo = sb("wk_lo", [P, DC, DH], F32R)
        wv_hi = sb("wv_hi", [P, DC, GD], F32R)
        wv_lo = sb("wv_lo", [P, DC, GD], F32R)
        wo_hi = sb("wo_hi", [P, 2, D], F32R)
        wo_lo = sb("wo_lo", [P, 2, D], F32R)
        oT_hi = sb("oT_hi", [P, 2, T], F32R)
        oT_lo = sb("oT_lo", [P, 2, T], F32R)
        wq_raw = sb("wq_raw", [P, DC, DH])
        wk_raw = sb("wk_raw", [P, DC, DH])
        wv_raw = sb("wv_raw", [P, GD])
        wo_raw = sb("wo_raw", [P, 2, D])
        bw_raw = sb("bw_raw", [P, DC, D])
        a_raw = sb("a_raw", [P, D])
        r_raw = sb("r_raw", [NR, D])
        b_raw = sb("b_raw", [P, DC, ER])
        y = sb("y", [P, NT, D])
        v = sb("v", [P, NT, GD])
        qT = sb("qT", [P, T])
        kT = sb("kT", [P, T])
        bias = sb("bias", [P, NB, S])
        madd = sb("madd", [P, NB, S])
        mask8 = sb("mask8", [P, NB, S], U8)
        some = sb("some", [P, NB])
        sc = sb("sc", [P, NB, S])
        pr = sb("pr", [P, NB, S])
        pT = sb("pT", [P, NT, P])
        mx = sb("mx", [P, NB])
        sm = sb("sm", [P, NB])
        rs = sb("rs", [P, NB])
        ident = sb("ident", [P, P])
        xn = sb("xn", [P, NX, D])
        st = sb("st", [P, NX, 6])
        mv = sb("mv", [P, NX, 2])
        ve = sb("ve", [P, NX])
        rstd = sb("rstd", [P, NX])
        shift = sb("shift", [P, NX])
        mhalf = sb("mhalf", [P, 1])
        warm = sb("warm", [P, 1])
        bb = sb("bb", [P, D])
        rb = sb("rb", [P, NR])
        mapi = sb("mapi", [P, NR], I32)
        mapf = sb("mapf", [P, NR])
        onehot = sb("onehot", [P, E, NR])
        lg = sb("lg", [P, NT, NR])
        lmax = sb("lmax", [P, NT])
        top = sb("top", [P, NT, 8])
        ex = sb("ex", [P, NT, NR])
        esum = sb("esum", [P, NT])
        rsum = sb("rsum", [P, NT])
        left = sb("left", [P, NT, NR])
        kept = sb("kept", [P, NT, NR])
        ew = sb("ew", [P, NRB, E, NR])
        we = sb("we", [P, NT, E])
        wn = sb("wn", [P, NT, E])
        hw = pT
        hwT_hi = sb("hwT_hi", [P, 2, P], F32R)
        hwT_lo = sb("hwT_lo", [P, 2, P], F32R)

        pP = [bank("pP0"), bank("pP1")]
        pY = [bank("pY0"), bank("pY1")]
        pS = bank("pS")
        pT_ = bank("pT_")
        pO = [bank("pO0"), bank("pO1")]
        pTurn = [pT_, pS, pO[0], pO[1]]

        pG = [pO[0], pO[1], pY[0], pY[1]]

        pF = [pP[0], pP[1], pO[0], pO[1]]
        pL = [pY[0], pY[1], pP[0], pP[1]]
        pW = [pY[0], pY[1], pY[0], pY[1], pP[0], pP[1], pS]

        fw = (wv_hi, wv_lo)
        last_oT = [t[:, 0:2 * T].rearrange("p (i t) -> p i t", i=2) for t in (cT_hi, cT_lo)]
        ar = [t[:, 2 * T:2 * T + DC * ARW].rearrange("p (c n) -> p c n", c=DC) for t in (cT_hi, cT_lo)]
        bt = [t[:, 2 * T + DC * ARW:2 * T + DC * ARW + D] for t in (cT_hi, cT_lo)]
        last_wo = [[w[:, :, :].rearrange("p c n -> p (c n)") for w in pair]
                   for pair in ((wq_hi, wk_hi), (wq_lo, wk_lo))]
        cTh = cT_hi[:, :].rearrange("p (c t) -> p c t", c=DC)
        cTl = cT_lo[:, :].rearrange("p (c t) -> p c t", c=DC)

        ld_ctx = [sem(f"ld_ctx{i}") for i in range(NT)]
        ld_x = [sem(f"ld_x{i}") for i in range(NT)]
        ld_wv0 = [sem(f"ld_wv0_{c}") for c in range(DC)]
        ld_wq, ld_wk, ld_wv, ld_wo = sem("ld_wq"), sem("ld_wk"), sem("ld_wv"), sem("ld_wo")
        ld_bias = sem("ld_bias")
        ld_mask, ld_small, ld_ffn = sem("ld_mask"), sem("ld_small"), sem("ld_ffn")
        stored = sem("stored")
        made0, made, mask_made, msk, sel_made = sem("made0"), sem("made"), sem("mask_made"), sem("msk"), sem("sel_made")
        warmed = sem("warmed")
        ln_step, ve_made, rstd_made, xn_made = sem("ln_step"), sem("ve_made"), sem("rstd_made"), sem("xn_made")
        shift_made, xn2_made = sem("shift_made"), sem("xn2_made")
        turned, turned_hi, turned_lo = sem("turned"), sem("turned_hi"), sem("turned_lo")
        wq_h, wq_l, wk_h, wk_l = sem("wq_h"), sem("wq_l"), sem("wk_h"), sem("wk_l")
        wv_h, wv_l, wo_h, wo_l = sem("wv_h"), sem("wv_l"), sem("wo_h"), sem("wo_l")
        proj_full, proj_free = sem("proj_full"), sem("proj_free")
        bias_made, s_full, s_read = sem("bias_made"), sem("s_full"), sem("s_read")
        sm_step, sub_made, exp_made, p_made = sem("sm_step"), sem("sub_made"), sem("exp_made"), sem("p_made")
        t_full, t_lower, t_upper = sem("t_full"), sem("t_lower"), sem("t_upper")
        o_full, o_hi, o_lo = sem("o_full"), sem("o_hi"), sem("o_lo")
        y_full, y_added = sem("y_full"), sem("y_added")
        fw_full, fw_hi, fw_lo = sem("fw_full"), sem("fw_hi"), sem("fw_lo")
        g_full, r_step, lg_made, ex_made, hw_made = (sem("g_full"), sem("r_step"), sem("lg_made"),
                                                     sem("ex_made"), sem("hw_made"))
        hwT_full, hwT_h, hwT_l = sem("hwT_full"), sem("hwT_h"), sem("hwT_l")
        yb_made, f_full, out_made = sem("yb_made"), sem("f_full"), sem("out_made")

        block = stack.enter_context(nc.Block())

        def has_next(last, s, ahead):
            return not last or s + ahead < GH

        def turn_of(step):
            n = TURNED.index(step)
            return n, pTurn[(0 if step[0] == "ctx" else 2) + step[1] % 2]

        def ffn_weight(n, part):
            src = pW[n]
            if n < DC:
                return fw[part][:, n, :], src[:, :]
            if n < DC + DC // 2:
                c = 2 * (n - DC)
                return (ar[part][:, c:c + 2, 0:ER + NR],
                        src[:, :].rearrange("p (c n) -> p c n", c=2)[:, :, 0:ER + NR])
            return bt[part], src[:, :]

        @block.sync
        def _(sp):
            def load_q(h):
                sp.dma_start(wq_raw[:, :, :], wq_d[:, :, bass.ds(h * DH, DH)]).then_inc(ld_wq, 16)

            def load_k(h):
                sp.dma_start(wk_raw[:, :, :], wk_d[:, :, bass.ds(h * DH, DH)]).then_inc(ld_wk, 16)

            def load_bias(h):
                for f in range(2):
                    for i in range(2):
                        sp.dma_start(bias[64 * f:64 * f + 64, i::2, :],
                                     bias_d[f, i, bass.ds(h, 1)].rearrange("o q j k -> (o q) j k")
                                     ).then_inc(ld_bias, 16)

            def load_wo(pair):
                sp.dma_start(wo_raw[:, :, :], wo_d[:, bass.ds(2 * pair, 2), :]).then_inc(ld_wo, 16)

            def load_ctx(t):
                sp.dma_start(v[:, t, :], ctx_d[:, t, :]).then_inc(ld_ctx[t], 16)

            def load_x(t):
                sp.dma_start(y[:, t, :], x_d[:, t, :]).then_inc(ld_x[t], 16)

            def load_wv0(c):
                sp.dma_start(bw_raw[:, c, :], wv_d[c, :, 0:GD]).then_inc(ld_wv0[c], 16)

            load_ctx(0)
            load_wv0(0)
            load_wv0(1)
            load_ctx(1)
            load_wv0(2)
            load_wv0(3)
            load_x(0)
            for t in range(2, NT):
                load_ctx(t)
                load_x(t - 1)
                if t == 4:
                    load_q(0)
                if t == 5:
                    load_k(0)
            load_x(NT - 1)
            for f in range(2):
                for i in range(2):
                    sp.dma_start(mask8[64 * f:64 * f + 64, i::2, :], mask_d[f, i]).then_inc(ld_mask, 16)
            load_bias(0)
            load_wo(0)
            sp.dma_start(bb[:, :], base_b.partition_broadcast(P)).then_inc(ld_small, 16)
            sp.dma_start(rb[:, :], router_b.partition_broadcast(P)).then_inc(ld_small, 16)
            sp.dma_start(mapi[:, :], emap.partition_broadcast(P)).then_inc(ld_small, 16)
            for h in (1, 2):
                sp.wait_ge(wq_l, h)
                load_q(h)
                sp.wait_ge(wk_l, h)
                load_k(h)

            def group(g, last=False):
                for s in range(GH):
                    h = g * GH + s
                    if not last:
                        sp.wait_ge(wv_l, g * GH + (s + GH))
                        sp.dma_start(wv_raw[:, :], wv_d[s, :, bass.ds((g + 1) * GD, GD)]).then_inc(ld_wv, 16)
                    if has_next(last, s, 1):
                        sp.wait_ge(s_read, h + 1)
                        load_bias(h + 1)
                    if has_next(last, s, 3):
                        sp.wait_ge(wq_l, h + 3)
                        load_q(h + 3)
                    if s % 2 and has_next(last, s, 1):
                        pair = g * 2 + s // 2
                        sp.wait_ge(wo_l, pair + 1)
                        load_wo(pair + 1)
                    if has_next(last, s, 3):
                        sp.wait_ge(wk_l, h + 3)
                        load_k(h + 3)
                    if last and s == 0:
                        sp.dma_start(bw_raw[:, :, :], bw_d).then_inc(ld_ffn, 16)
                        sp.dma_start(a_raw[:, :], a_d).then_inc(ld_ffn, 16)
                        sp.dma_start(r_raw[:, :], router_W).then_inc(ld_ffn, 16)
                        for o in range(DC):
                            sp.dma_start(b_raw[:, o, :].rearrange("p (e r) -> p e r", e=E),
                                         b_d[:, o]).then_inc(ld_ffn, 16)

            group(0)
            with sp.Fori(1, G - 1) as g:
                group(g)
            group(G - 1, last=True)
            for t in range(NT):
                sp.wait_ge(out_made, t + 1)
                sp.dma_start(out_d[:, t, :], y[:, t, :]).then_inc(stored, 16)
            sp.wait_ge(stored, 16 * NT)

        @block.gpsimd
        def _(pool):
            nc.gpsimd.memset(ident[:, :], 0.0).then_inc(made0, 1)
            pool.wait_ge(made0, 1)
            nc.gpsimd.affine_select(out=ident[:, :], in_=ident[:, :], compare_op=ALU.not_equal, fill=1.0,
                                    base=0, pattern=[[-1, P]], channel_multiplier=1).then_inc(made, 1)
            nc.gpsimd.memset(mhalf[:, :], -0.5).then_inc(made0, 1)
            pool.wait_ge(made0, 2)

            def rstd_of(n):
                pool.wait_ge(ve_made, n + 1)
                b = n % NX
                nc.gpsimd.tensor_tensor(rstd[:, b:b + 1], ve[:, b:b + 1], mhalf[:, :], ALU.pow).then_inc(rstd_made, 1)

            rstd_of(0)
            nc.gpsimd.memset(pT[:, :, :], 0.0).then_inc(made, 1)
            for t in range(1, NT):
                rstd_of(t)

            def add_mask(h):
                pool.wait_ge(ld_bias, (h + 1) * 64)
                nc.gpsimd.tensor_tensor(bias[:, :, :], bias[:, :, :], madd[:, :, :], ALU.add).then_inc(bias_made, 1)

            pool.wait_ge(mask_made, 1)
            for s in range(GH):
                add_mask(s)
            with pool.Fori(1, G) as g:
                for s in range(GH):
                    add_mask(g * GH + s)
            pool.wait_ge(ld_small, 48)
            for t in range(NT):
                b = t % NX
                if t >= NX:
                    pool.wait_ge(xn2_made, t - NX + 1)
                rstd_of(NT + t)
                pool.wait_ge(rstd_made, NT + t + 1)
                nc.gpsimd.tensor_scalar(shift[:, b:b + 1], mv[:, b, 0:1], rstd[:, b:b + 1], -1.0, ALU.mult,
                                        ALU.mult).then_inc(shift_made, 1)
            for t in range(NT):
                pool.wait_ge(xn2_made, t + 1)
                nc.gpsimd.tensor_tensor(y[:, t, :], y[:, t, :], bb[:, :], ALU.add).then_inc(yb_made, 1)

        @block.scalar
        def _(act):
            act.wait_ge(made0, 2)
            nc.scalar.activation(warm[:, :], mhalf[:, :], ACT.Exp).then_inc(warmed, 1)

            def copy_out(e, dst, src):
                act.wait_ge(proj_full, e + 1)
                nc.scalar.copy(dst, src).then_inc(proj_free, 1)

            def split_q(h):
                act.wait_ge(ld_wq, (h + 1) * 16)
                nc.scalar.copy(wq_hi[:, :, :], wq_raw[:, :, :]).then_inc(wq_h, 1)

            def split_k(h):
                act.wait_ge(ld_wk, (h + 1) * 16)
                nc.scalar.copy(wk_hi[:, :, :], wk_raw[:, :, :]).then_inc(wk_h, 1)

            def project_out(base, half, dst):
                e = base + half
                copy_out(e, dst[:, half % 2 * HALF:half % 2 * HALF + HALF], pP[half % 2][:, :])

            for step in OPENING:
                kind, i = step
                if step in PROJECTED:
                    e = PROJECTED.index(step)
                    cols = slice(i * HALF, (i + 1) * HALF)
                    dst = v[:, i, :] if kind == "v" else (qT if kind == "q" else kT)[:, cols]
                    copy_out(e, dst, pP[e % 2][:, :])
                    if step == ("k", 1):
                        split_k(1)
                    if step == ("q", 1):
                        split_q(1)
                    continue
                n, src = turn_of(step)
                dst = xT_hi if kind == "x" else cTh
                act.wait_ge(turned, n + 1)
                nc.scalar.copy(dst[:, :, i * P:(i + 1) * P], src[:, :].rearrange("p (c t) -> p c t", c=DC)
                               ).then_inc(turned_hi, 1)
                if step == ("ctx", 0):
                    for c in range(DC):
                        act.wait_ge(ld_wv0[c], 16)
                        nc.scalar.copy(wv_hi[:, c, :], bw_raw[:, c, :]).then_inc(wv_h, 1)
                if step == ("ctx", 4):
                    split_q(0)
                if step == ("ctx", 6):
                    split_k(0)

            def split_ffn(n):
                act.wait_ge(fw_full, n + 1)
                dst, src = ffn_weight(n, 0)
                if n == NFW - 1:
                    nc.scalar.mul(dst, src, LORA_SCALE).then_inc(fw_hi, 1)
                else:
                    nc.scalar.copy(dst, src).then_inc(fw_hi, 1)

            def group(g, last=False):
                for s in range(GH):
                    h = g * GH + s
                    base = g * PG + (P0 + 2 * NH * s)
                    act.wait_ge(sub_made, h + 1)
                    nc.scalar.activation(pr[:, :, :], sc[:, :, :], ACT.Exp).then_inc(exp_made, 1)
                    if has_next(last, s, 1):
                        project_out(base, 0, qT)
                        project_out(base, 1, qT)
                    act.wait_ge(t_full, h + 1)
                    nc.scalar.copy(pT[0:64, :, 0:64], pT_[0:64, :].rearrange("p (j q) -> p j q", q=64)
                                   ).then_inc(t_lower, 1)
                    if last and s == 1:
                        for n in range(2):
                            split_ffn(n)
                    if has_next(last, s, 2):
                        split_q(h + 2)
                    if not last:
                        act.wait_ge(ld_wv, g * 64 + 16 * (s + 1))
                        nc.scalar.copy(wv_hi[:, s, :], wv_raw[:, :]).then_inc(wv_h, 1)
                    if s % 2 and has_next(last, s, 1):
                        act.wait_ge(ld_wo, g * 32 + 16 * (s // 2 + 1))
                        nc.scalar.copy(wo_hi[:, :, :], wo_raw[:, :, :]).then_inc(wo_h, 1)
                    if has_next(last, s, 1):
                        project_out(base, 2, kT)
                        project_out(base, 3, kT)
                    if has_next(last, s, 2):
                        split_k(h + 2)
                    if last and s == 1:
                        for n in range(2, DC):
                            split_ffn(n)
                    if last and s == 2:
                        act.wait_ge(ld_wo, 16 * (H // 2))
                        for i in range(2):
                            ins = nc.scalar.copy(last_wo[0][i], wo_raw[:, i, :])
                        ins.then_inc(wo_h, 1)
                    if last and s == 3:
                        for n in range(DC, NFW):
                            split_ffn(n)
                    hi = last_oT[0] if last and s >= 2 else oT_hi
                    for i in range(NH):
                        act.wait_ge(o_full, h * 2 + (i + 1))
                        nc.scalar.copy(hi[:, s % 2, i * HALF:(i + 1) * HALF], pO[i][:, :]).then_inc(o_hi, 1)
                    if s == GH - 1 and not last:
                        for t in range(NT):
                            copy_out(g * PG + (P0 + GH * 2 * NH + t), v[:, t, :], pP[t % 2][:, :])

            group(0)
            with act.Fori(1, G - 1) as g:
                group(g)
            group(G - 1, last=True)

            for i in range(NT + 1):
                if i < NT:
                    b = i % NX
                    act.wait_ge(shift_made, i + 1)
                    if i >= NX:
                        act.wait_ge(turned, 2 * NT + i - NX + 1)
                    nc.scalar.activation(xn[:, b, :], y[:, i, :], ACT.Identity, scale=rstd[:, b:b + 1],
                                         bias=shift[:, b:b + 1]).then_inc(xn2_made, 1)
                if i >= 1:
                    t = i - 1
                    act.wait_ge(turned, 2 * NT + t + 1)
                    nc.scalar.copy(xT_hi[:, :, t * P:(t + 1) * P],
                                   pTurn[t % 2][:, :].rearrange("p (c t) -> p c t", c=DC)).then_inc(turned_hi, 1)
            for k in range(NT // NRB):
                act.wait_ge(lg_made, k + 1)
                tiles = slice(k * NRB, (k + 1) * NRB)
                nc.scalar.activation(ex[:, tiles, :], lg[:, tiles, :], ACT.Exp).then_inc(ex_made, 1)
            for t in range(NT):
                act.wait_ge(hwT_full, t + 1)
                nc.scalar.copy(hwT_hi[:, t % 2, :], pTurn[t % 2][:, 0:P]).then_inc(hwT_h, 1)

        @block.vector
        def _(dve):
            def lower(dst, src, hi, done):
                nc.vector.tensor_tensor(dst, src, hi.bitcast(F32), ALU.subtract).then_inc(done, 1)

            def split_q(h):
                dve.wait_ge(wq_h, h + 1)
                lower(wq_lo[:, :, :], wq_raw[:, :, :], wq_hi[:, :, :], wq_l)

            def split_k(h):
                dve.wait_ge(wk_h, h + 1)
                lower(wk_lo[:, :, :], wk_raw[:, :, :], wk_hi[:, :, :], wk_l)

            def sums(n, t):
                nc.vector.bn_stats(st[:, n % NX, :], y[:, t, :]).then_inc(ln_step, 1)

            def moments(n):
                dve.wait_ge(ln_step, 2 * n + 1)
                nc.vector.bn_aggr(mv[:, n % NX, :], st[:, n % NX, :]).then_inc(ln_step, 1)

            def add_eps(n):
                dve.wait_ge(ln_step, 2 * n + 2)
                b = n % NX
                nc.vector.tensor_scalar(ve[:, b:b + 1], mv[:, b, 1:2], EPS, None, ALU.add
                                        ).then_inc(ve_made, 1)

            def normalise(t):
                b = t % NX
                dve.wait_ge(rstd_made, t + 1)
                if t >= NX:
                    dve.wait_ge(turned, TURNED.index(("x", t - NX)) + 1)
                nc.vector.tensor_scalar(xn[:, b, :], y[:, t, :], mv[:, b, 0:1], rstd[:, b:b + 1],
                                        ALU.subtract, ALU.mult).then_inc(xn_made, 1)


            def prepare(t):
                dve.wait_ge(ld_x[t], 16)
                sums(t, t)
                moments(t)
                add_eps(t)

            for step in OPENING:
                kind, i = step
                if step in PROJECTED:
                    if kind == "v":
                        if i + 2 < NT:
                            prepare(i + 2)
                        if i + 1 < NT:
                            normalise(i + 1)
                    continue
                n, src = turn_of(step)
                hi, lo = (xT_hi, xT_lo) if kind == "x" else (cTh, cTl)
                dve.wait_ge(turned_hi, n + 1)
                lower(lo[:, :, i * P:(i + 1) * P], src[:, :].rearrange("p (c t) -> p c t", c=DC),
                      hi[:, :, i * P:(i + 1) * P], turned_lo)
                if step == ("ctx", 0):
                    for c in range(DC):
                        dve.wait_ge(wv_h, c + 1)
                        lower(wv_lo[:, c, :], bw_raw[:, c, :], wv_hi[:, c, :], wv_l)
                    prepare(0)
                    prepare(1)
                    normalise(0)
                if step == ("ctx", 4):
                    split_q(0)
                if step == ("ctx", 6):
                    split_k(0)
            dve.wait_ge(ld_mask, 64)
            nc.vector.tensor_scalar(madd[:, :, :], mask8[:, :, :], -NEG, NEG, ALU.mult, ALU.add).then_inc(mask_made, 1)
            nc.vector.tensor_reduce(some[:, :], mask8[:, :, :], AX.X, ALU.max).then_inc(msk, 1)
            dve.wait_ge(ld_small, 48)
            nc.vector.tensor_copy(mapf[:, :], mapi[:, :]).then_inc(msk, 1)
            dve.wait_ge(msk, 2)
            for e in range(E):
                nc.vector.tensor_scalar(onehot[:, e, :], mapf[:, :], float(e), None, ALU.is_equal).then_inc(sel_made, 1)
            split_k(1)
            split_q(1)

            def split_ffn(n):
                dve.wait_ge(fw_hi, n + 1)
                dst, src = ffn_weight(n, 1)
                hi, _ = ffn_weight(n, 0)
                if n == NFW - 1:
                    nc.vector.scalar_tensor_tensor(out=dst, in0=src, scalar=LORA_SCALE, in1=hi.bitcast(F32),
                                                   op0=ALU.mult, op1=ALU.subtract).then_inc(fw_lo, 1)
                else:
                    lower(dst, src, hi, fw_lo)

            last_pair = H // 2 - 1

            def add_tile(pair, t):
                dve.wait_ge(y_full, pair * NT + (t + 1))
                src = pL[t % 4] if isinstance(pair, int) and pair == last_pair else pY[t % 2]
                nc.vector.tensor_tensor(y[:, t, :], y[:, t, :], src[:, :], ALU.add).then_inc(y_added, 1)

            def group(g, first=False, last=False):
                for s in range(GH):
                    h = g * GH + s
                    step = h * 4
                    dve.wait_ge(s_full, h + 1)
                    dve.wait_ge(bias_made, h + 1)
                    nc.vector.scalar_tensor_tensor(out=sc[:, :, :], in0=pS[:, :].rearrange("p (b k) -> p b k", k=S),
                                                   scalar=SCALE, in1=bias[:, :, :], op0=ALU.mult,
                                                   op1=ALU.add).then_inc(s_read, 1)
                    dve.wait_ge(s_read, h + 1)
                    nc.vector.tensor_reduce(mx[:, :], sc[:, :, :], AX.X, ALU.max).then_inc(sm_step, 1)
                    dve.wait_ge(sm_step, step + 1)
                    nc.vector.tensor_tensor(sc[:, :, :], sc[:, :, :],
                                            mx[:, :].unsqueeze(2).to_broadcast([P, NB, S]),
                                            ALU.subtract).then_inc(sub_made, 1)
                    if last and s == 3:
                        for t in (4, 5):
                            add_tile(last_pair - 1, t)
                    dve.wait_ge(exp_made, h + 1)
                    nc.vector.tensor_reduce(sm[:, :], pr[:, :, :], AX.X, ALU.add).then_inc(sm_step, 1)
                    dve.wait_ge(sm_step, step + 2)
                    nc.vector.reciprocal(rs[:, :], sm[:, :]).then_inc(sm_step, 1)
                    dve.wait_ge(sm_step, step + 3)
                    nc.vector.tensor_tensor(rs[:, :], rs[:, :], some[:, :], ALU.mult).then_inc(sm_step, 1)
                    dve.wait_ge(sm_step, step + 4)
                    nc.vector.tensor_tensor(pr[:, :, :], pr[:, :, :],
                                            rs[:, :].unsqueeze(2).to_broadcast([P, NB, S]),
                                            ALU.mult).then_inc(p_made, 1)
                    if last and s == 3:
                        for t in (6, 7):
                            add_tile(last_pair - 1, t)
                    dve.wait_ge(t_full, h + 1)
                    nc.vector.tensor_copy(pT[64:128, :, 64:128], pT_[64:128, :].rearrange("p (j q) -> p j q", q=64)
                                          ).then_inc(t_upper, 1)
                    if last and s == 1:
                        for n in range(2):
                            split_ffn(n)
                    if has_next(last, s, 2):
                        split_q(h + 2)
                    if not last:
                        dve.wait_ge(wv_h, g * GH + (GH + s + 1))
                        lower(wv_lo[:, s, :], wv_raw[:, :], wv_hi[:, s, :], wv_l)
                    if s % 2 and has_next(last, s, 1):
                        dve.wait_ge(wo_h, g * 2 + (s // 2 + 1))
                        lower(wo_lo[:, :, :], wo_raw[:, :, :], wo_hi[:, :, :], wo_l)
                    if s % 2 == 0 and not (first and s == 0):
                        for t in range(4 if last and s == 2 else NT):
                            add_tile(g * 2 + (s // 2 - 1), t)
                    if has_next(last, s, 2):
                        split_k(h + 2)
                    if last and s == 1:
                        for n in range(2, DC):
                            split_ffn(n)
                    if last and s == 2:
                        dve.wait_ge(wo_h, last_pair + 1)
                        for i in range(2):
                            ins = nc.vector.tensor_tensor(last_wo[1][i], wo_raw[:, i, :], last_wo[0][i].bitcast(F32),
                                                          ALU.subtract)
                        ins.then_inc(wo_l, 1)
                    if last and s == 3:
                        for n in range(DC, NFW):
                            split_ffn(n)
                    hi, lo = last_oT if last and s >= 2 else (oT_hi, oT_lo)
                    for i in range(NH):
                        cols = slice(i * HALF, (i + 1) * HALF)
                        dve.wait_ge(o_hi, h * 2 + (i + 1))
                        lower(lo[:, s % 2, cols], pO[i][:, :], hi[:, s % 2, cols], o_lo)

            group(0, first=True)
            with dve.Fori(1, G - 1) as g:
                group(g)
            group(G - 1, last=True)

            dve.wait_ge(sel_made, E)
            for part in range(2):
                ins = nc.vector.memset(ar[part][:, :, ER + NR:ARW].bitcast(U32), 0)
            ins.then_inc(sel_made, 1)

            def chain(ins, n):
                ins.then_inc(r_step, 1)
                dve.wait_ge(r_step, n + 1)

            def two(bank_):
                return bank_[:, :].rearrange("p (t n) -> p t n", t=2)

            def route(k):
                n = k * RB
                tiles = slice(k * NRB, (k + 1) * NRB)
                dve.wait_ge(g_full, (k + 1) * NRB)
                for i in (2 * k, 2 * k + 1):
                    ins = nc.vector.tensor_tensor(lg[:, 2 * i:2 * i + 2, :], two(pG[i])[:, :, ER:ER + NR],
                                                  rb[:, :].unsqueeze(1).to_broadcast([P, 2, NR]), ALU.add)
                    chain(ins, n + i - 2 * k)
                chain(nc.vector.tensor_reduce(lmax[:, tiles], lg[:, tiles, :], AX.X, ALU.max), n + 2)
                nc.vector.tensor_tensor(lg[:, tiles, :], lg[:, tiles, :],
                                        lmax[:, tiles].unsqueeze(2).to_broadcast([P, NRB, NR]), ALU.subtract
                                        ).then_inc(lg_made, 1)
                dve.wait_ge(ex_made, k + 1)
                chain(nc.vector.tensor_reduce(esum[:, tiles], ex[:, tiles, :], AX.X, ALU.add), n + 3)
                for t in range(k * NRB, (k + 1) * NRB):
                    ins = nc.vector.max(top[:, t, :], ex[:, t, :])
                chain(ins, n + 4)
                nc.vector.reciprocal(rsum[:, tiles], esum[:, tiles]).then_inc(r_step, 1)
                for t in range(k * NRB, (k + 1) * NRB):
                    ins = nc.vector.match_replace(left[:, t, :], top[:, t, :], ex[:, t, :], -1.0)
                chain(ins, n + 6)
                chain(nc.vector.scalar_tensor_tensor(out=kept[:, tiles, :], in0=left[:, tiles, :], scalar=0.0,
                                                     in1=ex[:, tiles, :], op0=ALU.is_lt, op1=ALU.mult), n + 7)
                chain(nc.vector.tensor_tensor(ew[:, :, :, :], onehot[:, :, :].unsqueeze(1).to_broadcast([P, NRB, E, NR]),
                                              kept[:, tiles, :].unsqueeze(2).to_broadcast([P, NRB, E, NR]),
                                              ALU.mult), n + 8)
                chain(nc.vector.tensor_reduce(we[:, tiles, :], ew[:, :, :, :], AX.X, ALU.add), n + 9)
                chain(nc.vector.tensor_tensor(wn[:, tiles, :], we[:, tiles, :],
                                              rsum[:, tiles].unsqueeze(2).to_broadcast([P, NRB, E]), ALU.mult), n + 10)
                for t in range(k * NRB, (k + 1) * NRB):
                    nc.vector.tensor_tensor(hw[:, t, :].rearrange("p (e r) -> p e r", e=E),
                                            two(pG[t // 2])[:, t % 2, 0:ER].rearrange("p (e r) -> p e r", e=E),
                                            wn[:, t, :].unsqueeze(2).to_broadcast([P, E, R]), ALU.mult
                                            ).then_inc(hw_made, 1)

            add_tile(last_pair, 0)
            for i in range(NT + 3):
                if i < NT:
                    dve.wait_ge(y_added, last_pair * NT + i + 1)
                    sums(NT + i, i)
                    if i + 1 < NT:
                        add_tile(last_pair, i + 1)
                    if i >= NX:
                        dve.wait_ge(shift_made, i - NX + 1)
                    moments(NT + i)
                    add_eps(NT + i)
                if i >= 3:
                    t = i - 3
                    dve.wait_ge(turned_hi, 2 * NT + t + 1)
                    cols = slice(t * P, (t + 1) * P)
                    lower(xT_lo[:, :, cols], pTurn[t % 2][:, :].rearrange("p (c t) -> p c t", c=DC),
                          xT_hi[:, :, cols], turned_lo)
            for k in range(NT // NRB):
                route(k)
            for t in range(NT + 1):
                if t < NT:
                    dve.wait_ge(hwT_h, t + 1)
                    lower(hwT_lo[:, t % 2, :], pTurn[t % 2][:, 0:P], hwT_hi[:, t % 2, :], hwT_l)
                if t >= 1:
                    dve.wait_ge(f_full, t)
                    dve.wait_ge(yb_made, t)
                    nc.vector.tensor_tensor(y[:, t - 1, :], y[:, t - 1, :], pF[(t - 1) % 4][:, :], ALU.add
                                            ).then_inc(out_made, 1)

        @block.tensor
        def _(pe):
            def product(bank_, pairs, first=True, last=True):
                terms = [(a[i], b[j]) for a, b in pairs for i, j in ((0, 0), (1, 0), (0, 1))]
                for n, (a, b) in enumerate(terms):
                    mm = nc.tensor.matmul(bank_, a, b, start=first and n == 0, stop=last and n == len(terms) - 1)
                return mm

            def bank_free(e):
                if not isinstance(e, int) or e >= 2:
                    pe.wait_ge(proj_free, e - 1)

            def project(e, n, w, xt, half):
                bank_free(e)
                cols = slice(half * HALF, (half + 1) * HALF)
                product(pP[n][:, :], [((w[0][:, c, :], w[1][:, c, :]), (xt[0][:, c, cols], xt[1][:, c, cols]))
                                      for c in range(DC)]).then_inc(proj_full, 1)

            def v_tile(e, n, t, opening=False):
                bank_free(e)
                cols = slice(t * P, (t + 1) * P)
                for c in range(DC):
                    if opening:
                        pe.wait_ge(wv_l, c + 1)
                    mm = product(pP[n][:, :], [((cTh[:, c, cols], cTl[:, c, cols]), (wv_hi[:, c, :], wv_lo[:, c, :]))],
                                 first=c == 0, last=c == DC - 1)
                mm.then_inc(proj_full, 1)

            def turn(n, src, dst):
                for c in range(DC):
                    mm = nc.tensor.transpose(dst[:, c * P:(c + 1) * P], src[:, c * P:(c + 1) * P], ident[:, :])
                mm.then_inc(turned, 1)

            WQ, WK = (wq_hi, wq_lo), (wk_hi, wk_lo)
            XT, CT = (xT_hi, xT_lo), (cTh, cTl)

            pe.wait_ge(made, 1)
            for step in OPENING:
                kind, i = step
                if kind == "v":
                    pe.wait_ge(turned_lo, TURNED.index(("ctx", i)) + 1)
                    e = PROJECTED.index(step)
                    v_tile(e, e % 2, i, opening=i == 0)
                    continue
                if kind in ("q", "k"):
                    tile = ("x" if kind == "q" else "ctx", (i + 1) * (NT // 2) - 1)
                    pe.wait_ge(turned_lo, TURNED.index(tile) + 1)
                    pe.wait_ge(wq_l if kind == "q" else wk_l, 1)
                    e = PROJECTED.index(step)
                    project(e, e % 2, *((WQ, XT) if kind == "q" else (WK, CT)), i)
                    continue
                n, dst = turn_of(step)
                if i >= 2:
                    pe.wait_ge(turned_lo, TURNED.index((kind, i - 2)) + 1)
                if kind == "ctx":
                    pe.wait_ge(ld_ctx[i], 16)
                    turn(n, v[:, i, :], dst)
                else:
                    pe.wait_ge(xn_made, i + 1)
                    turn(n, xn[:, i % NX, :], dst)

            last_pair = H // 2 - 1

            def wo_terms(pair, t, i):
                cols = slice(t * P, (t + 1) * P)
                if isinstance(pair, int) and pair == last_pair:
                    return ([o[:, i, cols] for o in last_oT], [w[i] for w in last_wo])
                return ((oT_hi[:, i, cols], oT_lo[:, i, cols]), (wo_hi[:, i, :], wo_lo[:, i, :]))

            def times_wo(pair, t, heads=(0, 1)):
                dst = pL[t % 4] if isinstance(pair, int) and pair == last_pair else pY[t % 2]
                mm = product(dst[:, :], [wo_terms(pair, t, i) for i in heads],
                             first=heads[0] == 0, last=heads[-1] == 1)
                if heads[-1] == 1:
                    mm.then_inc(y_full, 1)

            def pair_times_wo(pair, tiles, free_at_first=False):
                for t in tiles:
                    if not (free_at_first and t < 2):
                        pe.wait_ge(y_added, pair * NT + (t - 1))
                    times_wo(pair, t)

            def group(g, first=False, last=False):
                for s in range(GH):
                    h = g * GH + s
                    base = g * PG + (P0 + 2 * NH * s)
                    if s == 0:
                        pe.wait_ge(proj_free, P0 - 1 if first else g * PG + (P0 - NT))
                    else:
                        pe.wait_ge(proj_free, base)
                    for half in range(2):
                        for b in [b for b in range(B) if b // 2 % 2 == half]:
                            blk = 2 * (b // 4) + b % 2
                            mm = nc.tensor.matmul(pS[64 * half:64 * half + 64, blk * S:(blk + 1) * S],
                                                  qT[:, b * S:(b + 1) * S], kT[:, b * S:(b + 1) * S],
                                                  start=True, stop=True)
                    mm.then_inc(s_full, 1)
                    if has_next(last, s, 1):
                        pe.wait_ge(wq_l, h + 2)
                        for half in range(NH):
                            project(base + half, half, WQ, XT, half)
                    elif last:
                        pair_times_wo(last_pair - 1, range(4, NT))
                    pe.wait_ge(p_made, h + 1)
                    for j in range(NB // 2):
                        mm = nc.tensor.transpose(pT_[:, j * P:(j + 1) * P],
                                                 pr[:, 2 * j:2 * j + 2, :].rearrange("p a k -> p (a k)"), ident[:, :])
                    mm.then_inc(t_full, 1)
                    if last and s == 1:
                        pe.wait_ge(y_added, (last_pair - 1) * NT)
                        ffn_weights(0, 2)
                    if has_next(last, s, 1):
                        pe.wait_ge(wk_l, h + 2)
                        for half in range(NH):
                            project(base + (NH + half), half, WK, CT, half)
                    if s % 2 == 0 and not (first and s == 0):
                        pair = g * 2 + (s // 2 - 1)
                        pe.wait_ge(wo_l, pair + 1)
                        pe.wait_ge(o_lo, h * 2)
                        pair_times_wo(pair, range(4 if last and s == 2 else NT), first and s == 2)
                    if last and s == 1:
                        ffn_weights(2, DC)
                    if last and s == 3:
                        ffn_weights(DC, NFW)
                    pe.wait_ge(t_lower, h + 1)
                    pe.wait_ge(t_upper, h + 1)
                    if not (first and s == 0):
                        pe.wait_ge(o_lo, h * 2)
                    if s == 0:
                        pe.wait_ge(proj_free, g * PG + P0)
                        if first:
                            pe.wait_ge(made, 2)
                    for i in range(NH):
                        for q in range(NT // 2):
                            t = i * (NT // 2) + q
                            mm = nc.tensor.matmul(pO[i][:, q * P:(q + 1) * P], v[:, t, s * DH:(s + 1) * DH],
                                                  pT[:, t, :], start=True, stop=True)
                        mm.then_inc(o_full, 1)
                    if s == GH - 1 and not last:
                        pe.wait_ge(wv_l, g * GH + 2 * GH)
                        for t in range(NT):
                            v_tile(g * PG + (P0 + GH * 2 * NH + t), t % 2, t)

            def ffn_weights(begin, end):
                pe.wait_ge(ld_ffn, 16 * (3 + DC))
                for n in range(begin, end):
                    dst = pW[n]
                    if n in (2, 3):
                        pe.wait_ge(fw_lo, n - 1)
                    elif n >= DC:
                        pe.wait_ge(proj_free, P0 + (G - 1) * PG + 3 * 2 * NH)
                    if n < DC:
                        for o in range(DC):
                            mm = nc.tensor.transpose(dst[:, o * P:(o + 1) * P], bw_raw[:, o, n * P:(n + 1) * P],
                                                     ident[:, :])
                    elif n < NFW - 1:
                        for i in range(2):
                            c = 2 * (n - DC) + i
                            nc.tensor.transpose(dst[:, i * ARW:i * ARW + ER], a_raw[:, c * P:(c + 1) * P],
                                                ident[:, :])
                            mm = nc.tensor.transpose(dst[:, i * ARW + ER:i * ARW + ER + NR],
                                                     r_raw[:, c * P:(c + 1) * P], ident[0:NR, 0:NR])
                    else:
                        for o in range(DC):
                            mm = nc.tensor.transpose(dst[:, o * P:(o + 1) * P], b_raw[:, o, :], ident[:, :])
                    mm.then_inc(fw_full, 1)

            group(0, first=True)
            with pe.Fori(1, G - 1) as g:
                group(g)
            group(G - 1, last=True)

            def turn_last(t):
                pe.wait_ge(xn2_made, t + 1)
                if t >= 2:
                    pe.wait_ge(turned_lo, 2 * NT + t - 1)
                turn(2 * NT + t, xn[:, t % NX, :], pTurn[t % 2])

            def xt_parts(t):
                cols = slice(t * P, (t + 1) * P)
                return [(xT_hi[:, c, cols], xT_lo[:, c, cols]) for c in range(DC)]

            def h_and_logits(t):
                pe.wait_ge(turned_lo, 2 * NT + t + 1)
                if t == 0:
                    pe.wait_ge(fw_lo, NFW)
                    pe.wait_ge(sel_made, E + 1)
                product(pG[t // 2][:, t % 2 * ARW:(t % 2 + 1) * ARW],
                        [(xt, (ar[0][:, c, :], ar[1][:, c, :])) for c, xt in enumerate(xt_parts(t))]
                        ).then_inc(g_full, 1)

            def base(t):
                if t >= 4:
                    pe.wait_ge(out_made, t - 3)
                elif t >= 2:
                    pe.wait_ge(hw_made, NRB)
                product(pF[t % 4][:, :], [(xt, (fw[0][:, c, :], fw[1][:, c, :])) for c, xt in enumerate(xt_parts(t))],
                        last=False)

            def turn_hw(t):
                pe.wait_ge(hw_made, t + 1)
                if t >= 2:
                    pe.wait_ge(hwT_l, t - 1)
                nc.tensor.transpose(pTurn[t % 2][:, 0:P], hw[:, t, :], ident[:, :]).then_inc(hwT_full, 1)

            def lora(t):
                pe.wait_ge(hwT_l, t + 1)
                product(pF[t % 4][:, :], [((hwT_hi[:, t % 2, :], hwT_lo[:, t % 2, :]), bt)], first=False
                        ).then_inc(f_full, 1)

            pe.wait_ge(wo_l, last_pair + 1)
            pe.wait_ge(y_added, last_pair * NT)
            for t in range(4):
                if t == 2:
                    pe.wait_ge(fw_lo, NFW)
                times_wo(last_pair, t, heads=(0,))
            pe.wait_ge(o_lo, 2 * H)
            for t in range(4):
                times_wo(last_pair, t, heads=(1,))
            for i in range(4, NT + 6):
                if i < NT:
                    pe.wait_ge(y_added, last_pair * NT + (i - 3))
                    times_wo(last_pair, i)
                if 4 <= i < NT + 4:
                    turn_last(i - 4)
                if i >= 6:
                    h_and_logits(i - 6)
                    if i == NT + 1:
                        pe.wait_ge(y_added, (last_pair + 1) * NT)
            for i in range(NT + 2):
                if i < NT:
                    base(i)
                if i == 1:
                    turn_hw(0)
                    turn_hw(1)
                if i >= 2:
                    lora(i - 2)
                    if i < NT:
                        turn_hw(i)


_INS = ["x", "ctx_4096", "fside_Bx32xSxS2_0", "mask_BxSxS2_bk0", "L0_xattn_Wq", "L0_xattn_Wk", "L0_xattn_Wv",
        "L0_xattn_Wo", "L0_ffn_base_W", "L0_ffn_base_b", "L0_ffn_router_W", "L0_ffn_router_b", "L0_ffn_A",
        "L0_ffn_B", "L0_ffn_expert_map"]


def kernel(**inputs):
    import numpy as _np
    import concourse.bacc as _bacc
    from concourse import mybir as _mybir
    from concourse.bass_utils import run_bass_kernel_spmd as _run

    nc = _bacc.Bacc("TRN2", target_bir_lowering=False, num_devices=1)
    arrays, args = {}, []
    for name in _INS:
        a = _np.ascontiguousarray(inputs[name])
        arrays[f"in_{name}"] = a
        args.append(nc.dram_tensor(f"in_{name}", a.shape, _mybir.dt.from_np(a.dtype), kind="ExternalInput").ap())
    out = nc.dram_tensor("out_0", (B, S, D), _mybir.dt.float32, kind="ExternalOutput").ap()
    xattn_ffn(nc, *args, out)
    r = _run(nc, [arrays], core_ids=[0])
    return r.results[0]["out_0"]
```
